# Optimizing a Trainium2 kernel written in Bass

```python
import numpy as np
import jax
import jax.numpy as jnp

def _softmax(x, axis=-1):
    return jax.nn.softmax(x, axis=axis)

def _gelu(x):
    return jax.nn.gelu(x, approximate=True)

def _silu(x):
    return jax.nn.silu(x)

def _sigmoid(x):
    return jax.nn.sigmoid(x)

def _layernorm(x, axis=-1, eps=1e-05):
    m = jnp.mean(x, axis=axis, keepdims=True)
    v = jnp.var(x, axis=axis, keepdims=True)
    return (x - m) / jnp.sqrt(v + eps)

def _scatter_add(tgt, idx, src, axis=0):
    return tgt.at[idx].add(src)

def _segment_sum(src, seg, n):
    return jax.ops.segment_sum(src, seg, n)
kernel_name = 'mk_seq_postln_d1_jaxref_r4_2e2900'

def setup_inputs(seed: int=0):
    np.random.seed(seed)
    _w = jnp.asarray

    def _L0_attn_setup():
        import jax, jax.numpy as jnp
        import numpy as np
        D_MODEL = 256
        N_HEADS = 16
        D_K = D_MODEL // N_HEADS
        D_V = D_MODEL // N_HEADS
        key = jax.random.key(seed)
        ks = jax.random.split(key, 9)
        B, S = (4, 512)
        s = 1.0 / np.sqrt(D_MODEL)
        return {'x': jax.random.normal(ks[0], (B, S, D_MODEL), dtype=jnp.float32), 'w_q': jax.random.uniform(ks[1], (D_MODEL, N_HEADS * D_K), jnp.float32, -s, s), 'b_q': jax.random.uniform(ks[2], (N_HEADS * D_K,), jnp.float32, -s, s), 'w_k': jax.random.uniform(ks[3], (D_MODEL, N_HEADS * D_K), jnp.float32, -s, s), 'b_k': jax.random.uniform(ks[4], (N_HEADS * D_K,), jnp.float32, -s, s), 'w_v': jax.random.uniform(ks[5], (D_MODEL, N_HEADS * D_V), jnp.float32, -s, s), 'b_v': jax.random.uniform(ks[6], (N_HEADS * D_V,), jnp.float32, -s, s), 'w_o': jax.random.uniform(ks[7], (N_HEADS * D_V, D_MODEL), jnp.float32, -s, s), 'b_o': jax.random.uniform(ks[8], (D_MODEL,), jnp.float32, -s, s)}
    _L0_attn_in = _L0_attn_setup()

    def _L0_ffn_setup():
        import jax, jax.numpy as jnp
        import numpy as np
        B, T, C, I, E = (4, 512, 256, 704, 7)

        def _swiglu(h, w1, w2, w3):
            return jax.nn.silu(h @ w1.T) * (h @ w3.T) @ w2.T
        key = jax.random.key(seed)
        ks = jax.random.split(key, 9)
        sc_c = 1.0 / np.sqrt(C)
        sc_i = 1.0 / np.sqrt(I)
        return {'x': jax.random.normal(ks[0], (B, T, C), jnp.float32), 'router_w': jax.random.normal(ks[1], (E, C), jnp.float32) * sc_c, 'routing_bias': jnp.zeros((E,), jnp.float32), 'sw1': jax.random.normal(ks[2], (I, C), jnp.float32) * sc_c, 'sw2': jax.random.normal(ks[3], (C, I), jnp.float32) * sc_i, 'sw3': jax.random.normal(ks[4], (I, C), jnp.float32) * sc_c, 'ew1': jax.random.normal(ks[5], (E, I, C), jnp.float32) * sc_c, 'ew2': jax.random.normal(ks[6], (E, C, I), jnp.float32) * sc_i, 'ew3': jax.random.normal(ks[7], (E, I, C), jnp.float32) * sc_c}
    _L0_ffn_in = _L0_ffn_setup()
    _d = {'L0_attn_x': _L0_attn_in['x'], 'L0_attn_w_q': _L0_attn_in['w_q'], 'L0_attn_b_q': _L0_attn_in['b_q'], 'L0_attn_w_k': _L0_attn_in['w_k'], 'L0_attn_b_k': _L0_attn_in['b_k'], 'L0_attn_w_v': _L0_attn_in['w_v'], 'L0_attn_b_v': _L0_attn_in['b_v'], 'L0_attn_w_o': _L0_attn_in['w_o'], 'L0_attn_b_o': _L0_attn_in['b_o'], 'L0_ffn_router_w': _L0_ffn_in['router_w'], 'L0_ffn_routing_bias': _L0_ffn_in['routing_bias'], 'L0_ffn_sw1': _L0_ffn_in['sw1'], 'L0_ffn_sw2': _L0_ffn_in['sw2'], 'L0_ffn_sw3': _L0_ffn_in['sw3'], 'L0_ffn_ew1': _L0_ffn_in['ew1'], 'L0_ffn_ew2': _L0_ffn_in['ew2'], 'L0_ffn_ew3': _L0_ffn_in['ew3']}
    _x0 = _d['L0_attn_x']
    _d['L0_attn_x'] = jax.random.normal(jax.random.fold_in(jax.random.key(seed), 1), (8, 512, 256), dtype=_x0.dtype)
    del _x0
    return _d

def reference(L0_attn_x, L0_attn_w_q, L0_attn_b_q, L0_attn_w_k, L0_attn_b_k, L0_attn_w_v, L0_attn_b_v, L0_attn_w_o, L0_attn_b_o, L0_ffn_router_w, L0_ffn_routing_bias, L0_ffn_sw1, L0_ffn_sw2, L0_ffn_sw3, L0_ffn_ew1, L0_ffn_ew2, L0_ffn_ew3):

    def _L0_attn_ref(x, w_q, b_q, w_k, b_k, w_v, b_v, w_o, b_o):
        import jax, jax.numpy as jnp
        import numpy as np
        D_MODEL = 256
        N_HEADS = 16
        D_K = D_MODEL // N_HEADS
        D_V = D_MODEL // N_HEADS
        B, S, _ = x.shape

        def split_heads(t, d):
            return t.reshape(B, S, N_HEADS, d).transpose(0, 2, 1, 3)
        q = split_heads(x @ w_q + b_q, D_K)
        k = split_heads(x @ w_k + b_k, D_K)
        v = split_heads(x @ w_v + b_v, D_V)
        scale = 1.0 / jnp.sqrt(jnp.asarray(D_K, x.dtype))
        scores = jnp.einsum('bhsd,bhtd->bhst', q, k) * scale
        causal = jnp.triu(jnp.ones((S, S), dtype=bool), k=1)
        scores = jnp.where(causal, -jnp.inf, scores)
        attn = jax.nn.softmax(scores, axis=-1)
        out = jnp.einsum('bhst,bhtd->bhsd', attn, v)
        out = out.transpose(0, 2, 1, 3).reshape(B, S, N_HEADS * D_V)
        return out @ w_o + b_o

    def _L0_ffn_ref(x, router_w, routing_bias, sw1, sw2, sw3, ew1, ew2, ew3):
        import jax, jax.numpy as jnp
        import numpy as np
        B, T, C, I, E = (4, 512, 256, 704, 7)

        def _swiglu(h, w1, w2, w3):
            return jax.nn.silu(h @ w1.T) * (h @ w3.T) @ w2.T
        b, t, c = x.shape
        shared_out = _swiglu(x, sw1, sw2, sw3)
        logits = jnp.clip(x @ router_w.T + routing_bias, -50.0, 50.0)
        probs = jax.nn.sigmoid(logits)
        num_switched = 1
        topk_probs, topk_idx = jax.lax.top_k(probs, num_switched)
        topk_probs = jnp.clip(topk_probs, 1e-08, 1.0 - 1e-08)
        xf = x.reshape(-1, c)
        sel = topk_idx.reshape(-1)
        p = topk_probs.reshape(-1)
        switched = jnp.zeros_like(xf)
        n_experts = ew1.shape[0]
        for e in range(n_experts):
            y = _swiglu(xf, ew1[e], ew2[e], ew3[e])
            w = jnp.where(sel == e, p, 0.0)
            switched = switched + w[:, None] * y
        switched = switched.reshape(b, t, c)
        total_weight = 0.5 + topk_probs.sum(axis=-1)
        total_weight = jnp.clip(total_weight[..., None] + 1e-08, 0.5, 2.0)
        return 0.5 / total_weight * shared_out + switched / total_weight
    x = L0_attn_x
    x = _layernorm(x + _L0_attn_ref(x, L0_attn_w_q, L0_attn_b_q, L0_attn_w_k, L0_attn_b_k, L0_attn_w_v, L0_attn_b_v, L0_attn_w_o, L0_attn_b_o), axis=-1)
    x = _layernorm(x + _L0_ffn_ref(x, L0_ffn_router_w, L0_ffn_routing_bias, L0_ffn_sw1, L0_ffn_sw2, L0_ffn_sw3, L0_ffn_ew1, L0_ffn_ew2, L0_ffn_ew3), axis=-1)
    return x

_drawn_inputs = setup_inputs


def setup_inputs(seed=0):
    import zlib

    import numpy as np

    out = dict(_drawn_inputs(seed))
    spreads = {'L0_ffn_routing_bias': (0.0, 0.1)}
    factors = {'L0_attn_b_q': 5.827, 'L0_attn_b_k': 8.0}
    for name, (base, spread) in spreads.items():
        noise = np.random.default_rng([zlib.crc32(name.encode()), seed]).standard_normal(out[name].shape)
        drawn = base * np.exp(spread * noise) if base else spread * noise
        out[name] = jnp.asarray(drawn.astype(out[name].dtype))
    for name, factor in factors.items():
        out[name] = (out[name] * factor).astype(out[name].dtype)
    return out
```

```python
from contextlib import ExitStack

import concourse.bass as bass
from concourse import mybir

ALU = mybir.AluOpType
ACT = mybir.ActivationFunctionType
AX_X = mybir.AxisListType.X
F32 = mybir.dt.float32
BF16 = mybir.dt.bfloat16
I32 = mybir.dt.int32
U32 = mybir.dt.uint32

P = 128
B, S, D = 8, 512, 256
H, DH = 16, 16
TOK = B * S
TT = TOK // P
NT = S // P
KD = D // P
QH = 4
NQ = H // QH
QUADS = B * NQ
I, E = 704, 7
NW = E + 1
UP = 2 * I
KI = -(-I // P)
LAST = I - (KI - 1) * P
UPW, DNW = KD * UP, KI * D
SLOT = UPW + DNW
PIECE = I // 2
RT = TT + E
SORTED = RT * P
SCALE = 0.25
EPS = 1e-5
MASKED = -1e30
K_PARTS = (0, 0, 1, 1, 0, 2)
Q_PARTS = (0, 1, 0, 1, 2, 0)
NP_ = len(K_PARTS)
SR = NP_ * DH
SM = SR + 3


def wait(eng, sem, count):
    if not isinstance(count, int) or count > 0:
        eng.wait_ge(sem, count)


def block_kernel(nc, x, w_qkv, b_qk, b_v, w_o, b_o, w_r, b_r, w_sets, out):
    with ExitStack() as ctx:
        def sb(name, shape, dt=F32):
            return ctx.enter_context(nc.sbuf_tensor(name, shape, dt))

        def sem(name):
            return ctx.enter_context(nc.semaphore(name))

        qk_parts = nc.dram_tensor("qk_parts", [2, 3, QUADS * QH * DH, S], BF16, kind="Internal").ap()
        rows_in = nc.dram_tensor("rows_in", [TOK + SORTED, D], F32, kind="Internal").ap()
        rows_out = nc.dram_tensor("rows_out", [TOK + SORTED, D], F32, kind="Internal").ap()

        weights = sb("weights", [P, NW * SLOT])
        res = sb("res", [P, TT, D])
        work = sb("work", [P, 6144])
        EARLY = 4
        place = [EARLY * SLOT]

        def carve(words):
            at = place[0]
            place[0] += words
            assert place[0] <= NW * SLOT
            return weights[:, at:at + words]

        v_all = carve(B * NT * D).rearrange("p (b n c) -> p b n c", b=B, n=NT)
        shared_at = place[0]
        x_in = [carve(NT * D).rearrange("p (n c) -> p n c", n=NT) for _ in range(2)]
        xT = [carve(KD * S).rearrange("p (k n) -> p k n", k=KD) for _ in range(2)]
        qk32 = [carve(S) for _ in range(2)]
        rest = [carve(S) for _ in range(2)]
        parts = [carve(3 * S // 2).bitcast(BF16).rearrange("p (t n) -> p t n", t=3) for _ in range(2)]
        wqkv = carve(KD * 3 * D).rearrange("p (k n) -> p k n", k=KD)
        place[0] = shared_at
        q_st = [carve(QH * S // 2).bitcast(BF16).rearrange("p (h n) -> p h n", h=QH) for _ in range(NQ)]
        k_st = [carve(QH * S // 2).bitcast(BF16).rearrange("p (h n) -> p h n", h=QH) for _ in range(NQ)]
        place[0] = EARLY * SLOT
        RING = 4
        att_in = [carve(D) for _ in range(RING)]
        attT = [carve(D).rearrange("p (k n) -> p k n", k=KD) for _ in range(RING)]
        x_res = [carve(D) for _ in range(RING)]
        xb = [carve(D) for _ in range(RING)]
        hid = [carve(D) for _ in range(RING)]
        x1 = [carve(D) for _ in range(RING)]
        x1T = [carve(D).rearrange("p (k n) -> p k n", k=KD) for _ in range(RING)]

        y_own = weights[:, 0:TT * D].rearrange("p (t c) -> p t c", t=TT)

        probs = work[:, 0:4096].rearrange("p (j h n) -> p j h n", j=2, h=QH)
        o_sb = work[:, 4096:4608]
        v_ext = [work[:, 4608 + 512 * i:5120 + 512 * i].rearrange("p (n h d) -> p n h d", n=NT, h=QH) for i in range(2)]
        f_x = [work[:, 256 * i:256 * (i + 1)] for i in range(2)]
        f_xT = [work[:, 512 + 256 * i:768 + 256 * i].rearrange("p (k n) -> p k n", k=KD) for i in range(2)]
        f_s = work[:, 1024:1024 + I]
        f_h = [work[:, 1728 + I * i:1728 + I * (i + 1)] for i in range(2)]
        f_hT = [work[:, 3136 + KI * P * i:3136 + KI * P * (i + 1)].rearrange("p (k n) -> p k n", k=KI) for i in range(2)]
        f_y = [work[:, 4672 + 256 * i:4928 + 256 * i] for i in range(2)]

        ident = sb("ident", [P, P])
        ident_bf = sb("ident_bf", [P, P], BF16)
        zeros = sb("zeros", [P, D])
        ones = sb("ones", [P, P])
        mask_q = sb("mask_q", [P, P], BF16)
        mask_k = sb("mask_k", [P, P], BF16)
        before = sb("before", [P, P], BF16)
        ones_bf = sb("ones_bf", [P, P], BF16)
        bqk = sb("bqk", [P, 4])
        bv = sb("bv", [P, D])
        bo = sb("bo", [P, D])
        wo = sb("wo", [P, KD, D])
        wr = sb("wr", [P, KD, E])
        br = sb("br", [P, E])
        negmax = [sb(f"negmax{i}", [P, QH * NT]) for i in range(2)]
        m_rest = sb("m_rest", [P, QH * NT])
        m_parts = sb("m_parts", [P, P], BF16)
        m_rows = sb("m_rows", [3 * QH * NT, P], BF16)
        rden = sb("rden", [P, NT * QH])
        stats = [sb(f"stats{i}", [P, 8]) for i in range(RING)]
        std = [sb(f"std{i}", [P, 1]) for i in range(RING)]
        eps = sb("eps", [P, 1])
        rstd = [sb(f"rstd{i}", [P, 1]) for i in range(RING)]
        TE = TT * E
        grid = lambda t: t.rearrange("p (t e) -> p t e", t=TT)
        route = [grid(carve(TT * E)) for _ in range(6)]
        onehot_bf = carve(TT * E // 2).bitcast(BF16)
        col = [carve(TT) for _ in range(4)]
        share = sb("share", [P, TT])
        gate = sb("gate", [P, TT])
        pos = sb("pos", [P, TT], U32)
        need = carve(E * TT).rearrange("p (e t) -> p e t", e=E)
        step128 = carve(E * TT).rearrange("p (e t) -> p e t", e=E)
        tiles_of = [sb(f"tiles_of{i}", [P, E]) for i in range(2)]
        tile_no = carve(RT * E)[0:1].rearrange("p (t e) -> p t e", t=RT)
        tile_ge = carve(RT * E)[0:1].rearrange("p (t e) -> p t e", t=RT)
        tile_e = sb("tile_e", [1, RT])
        tile_expert = sb("tile_expert", [1, RT], I32)

        ps = ctx.enter_context(nc.psum_tensor("ps", [P, 8, 512], F32))

        consts_in = sem("consts_in")
        wqkv_in = sem("wqkv_in")
        consts_made = sem("consts_made")
        pool_step = sem("pool_step")
        x_loaded = [sem(f"x_loaded{i}") for i in range(2)]
        x_turned = sem("x_turned")
        xT_copied = sem("xT_copied")
        qk_projected = sem("qk_projected")
        v_projected = sem("v_projected")
        qk_read = sem("qk_read")
        rest_made = sem("rest_made")
        mid_made = sem("mid_made")
        low_made = sem("low_made")
        v_kept = sem("v_kept")
        parts_stored = [sem(f"parts_stored{i}") for i in range(2)]
        stack_loaded = [sem(f"stack_loaded{i}") for i in range(NQ)]
        ones_rows = sem("ones_rows")
        max_scored = sem("max_scored")
        max_found = sem("max_found")
        m_step = sem("m_step")
        m_split = sem("m_split")
        m_turned = sem("m_turned")
        m_copied = sem("m_copied")
        m_placed = sem("m_placed")
        scored = sem("scored")
        exped = sem("exped")
        v_ready = sem("v_ready")
        pv_done = sem("pv_done")
        o_copied = sem("o_copied")
        o_turned = sem("o_turned")
        rden_made = sem("rden_made")
        att_kept = sem("att_kept")
        w_loaded = [sem(f"w_loaded{i}") for i in range(2)]
        zero_rows = sem("zero_rows")
        x_res_in = [sem(f"x_res_in{i}") for i in range(RING)]
        att_staged = sem("att_staged")
        xb_made = sem("xb_made")
        att_turned = sem("att_turned")
        attT_copied = sem("attT_copied")
        out_projected = sem("out_projected")
        sum_made = sem("sum_made")
        stats_made = sem("stats_made")
        var_made = sem("var_made")
        rstd_made = sem("rstd_made")
        std_made = sem("std_made")
        x1_made = sem("x1_made")
        x1_kept = sem("x1_kept")
        x1_stored = [sem(f"x1_stored{i}") for i in range(RING)]
        x1_turned = sem("x1_turned")
        x1T_copied = sem("x1T_copied")
        logits_made = sem("logits_made")
        iotas_made = sem("iotas_made")
        logits_clipped = sem("logits_clipped")
        probs_made = sem("probs_made")
        onehot_made = sem("onehot_made")
        counted = sem("counted")
        route_step = sem("route_step")
        routed = sem("routed")
        scattered = sem("scattered")
        fx_loaded = [sem(f"fx_loaded{i}") for i in range(2)]
        fx_turned = sem("fx_turned")
        fxT_copied = sem("fxT_copied")
        gate_up = sem("gate_up")
        lin_up = sem("lin_up")
        silu_made = sem("silu_made")
        h_made = sem("h_made")
        h_turned = sem("h_turned")
        hT_copied_a = sem("hT_copied_a")
        hT_copied_v = sem("hT_copied_v")
        y_made = sem("y_made")
        y_copied = sem("y_copied")
        y_stored = [sem(f"y_stored{i}") for i in range(2)]
        gathered = [sem(f"gathered{i}") for i in range(RING)]
        ysh_in = [sem(f"ysh_in{i}") for i in range(RING)]
        shared_added = sem("shared_added")
        fin_made = sem("fin_made")
        out_stored = [sem(f"out_stored{i}") for i in range(RING)]

        qk_rows = QH * DH
        qk_store = qk_parts.rearrange("w t r n -> w r t n")

        block = ctx.enter_context(nc.Block())

        U = 2 * NT
        STEPS = NQ * U
        M_TURN, S_LAG = 9, 12
        PV_LAG, O_COPY, O_TURN = S_LAG + 3, S_LAG + 10, S_LAG + 11

        def item(b, s, lag):
            d, n = divmod(s - lag, STEPS)
            if isinstance(b, int) and not 0 <= b + d < B:
                return None
            if lag == 0 and d < 0:
                return None
            return b + d, n

        CT = 8
        PROJ_LAG, NORM_LAG, STORE_LAG, X1_LAG, LOGIT_LAG = 1, 2, 3, 4, 5

        def tile_rounds(eng, body):
            def one(b):
                for s in range(CT):
                    def at(lag, b=b, s=s):
                        d, n = divmod(s - lag, CT)
                        if isinstance(b, int) and not 0 <= b + d < TT // CT:
                            return None
                        return (b + d) * CT + n, n, b + d
                    body(at)
            one(0)
            with eng.Fori(1, TT // CT) as b:
                one(b)
            one(TT // CT)

        FT = TT + RT
        UP_LAG, DOWN_LAG = 1, 2
        STEADY = 4

        def ffn_steps(eng, body, last_lag):
            def one(s, par, first):
                body(s, par, lambda lag: first - lag < TT)
            end = FT // 2 * 2
            for s in range(STEADY):
                one(s, s % 2, s)
            with eng.Fori(STEADY // 2, TT // 2) as i:
                for par in range(2):
                    one(2 * i + par, par, STEADY + par)
            for s in range(TT, TT + STEADY):
                one(s, s % 2, s)
            with eng.Fori((TT + STEADY) // 2, end // 2) as i:
                for par in range(2):
                    one(2 * i + par, par, TT + STEADY + par)
            for s in range(end, FT + last_lag):
                one(s, s % 2, s)

        def inside(s, lag):
            return not isinstance(s, int) or 0 <= s - lag < FT

        def final_rounds(eng, body):
            for r in range(RING):
                body(r, r, 0)
            with eng.Fori(1, TT // RING) as i:
                for r in range(RING):
                    body(RING * i + r, r, i)

        def rounds(eng, body):
            def one(b):
                for s in range(STEPS):
                    body(b, s)
            one(0)
            with eng.Fori(1, B) as b:
                one(b)
            one(B)

        @block.sync
        def _(sp):
            for dst, src in ((bqk, b_qk), (bv, b_v), (bo, b_o), (br, b_r)):
                sp.dma_start(dst[:], src).then_inc(consts_in, 16)
            sp.dma_start(wo[:], w_o).then_inc(consts_in, 16)
            sp.dma_start(wr[:], w_r).then_inc(consts_in, 16)
            sp.dma_start(wqkv, w_qkv).then_inc(wqkv_in, 16)
            sp.wait_ge(pool_step, 5)
            sp.dma_start(rows_in[TOK:TOK + SORTED].rearrange("(t p) c -> p t c", p=P),
                         zeros[:].unsqueeze(1).broadcast_to([P, RT, D])).then_inc(zero_rows, 16)

            def proj_batch(i, par):
                b = 2 * i + par
                wait(sp, x_turned, b - 1)
                sp.dma_start(x_in[par], x[bass.ds(b * NT, NT)].rearrange("n p c -> p n c")).then_inc(x_loaded[par], 16)

            def store_batch(b):
                for m in range(4):
                    sp.wait_ge(low_made, 4 * b + m + 1)
                    sp.dma_start(qk_store[m // 2, bass.ds((4 * b + 2 * (m % 2)) * qk_rows, P)],
                                 parts[m % 2]).then_inc(parts_stored[m % 2], 16)

            proj_batch(0, 0)
            proj_batch(0, 1)
            store_batch(0)
            with sp.Fori(1, B // 2) as i:
                proj_batch(i, 0)
                store_batch(2 * i - 1)
                proj_batch(i, 1)
                store_batch(2 * i)
            store_batch(B - 1)

            def load_stack(b, q):
                wait(sp, scored, U * (NQ * b + q - NQ + 1))
                for t in range(NP_):
                    for side, st, which in ((0, q_st, Q_PARTS), (1, k_st, K_PARTS)):
                        src = qk_parts[side, which[t], bass.ds((NQ * b + q) * qk_rows, qk_rows)]
                        sp.dma_start(st[q][t * DH:(t + 1) * DH], src.rearrange("(h d) n -> d h n", h=QH)
                                     ).then_inc(stack_loaded[q], 16)

            def place_max(b, q):
                sp.wait_ge(m_copied, NQ * b + q + 1)
                sp.dma_start(q_st[q][SR:SM].rearrange("p h n -> p (h n)"), m_rows[:]).then_inc(m_placed, 16)

            for i in range(2):
                sp.wait_ge(parts_stored[i], 16 * 2 * B)
            sp.wait_ge(v_projected, B)
            load_stack(0, 0)
            load_stack(0, 1)

            def stacks(b):
                for q in range(NQ):
                    if q < 2:
                        load_stack(b, q + 2)
                    elif not (isinstance(b, int) and b == B - 1):
                        load_stack(b + 1, q - 2)
                    place_max(b, q)

            stacks(0)
            with sp.Fori(1, B - 1) as b:
                stacks(b)
            stacks(B - 1)
            sp.wait_ge(att_kept, QUADS)

            def residual(at):
                if t := at(0):
                    T, n, _ = t
                    wait(sp, xb_made, T - RING + 1)
                    sp.dma_start(x_res[n % RING], x[bass.ds(T, 1)].rearrange("o p c -> (o p) c")
                                 ).then_inc(x_res_in[n % RING], 16)
                if t := at(STORE_LAG):
                    T, n, _ = t
                    sp.wait_ge(x1_made, T + 1)
                    sp.dma_start(rows_in[bass.ds(T * P, P)], x1[n % RING]).then_inc(x1_stored[n % RING], 16)

            tile_rounds(sp, residual)

            for r in range(RING):
                sp.wait_ge(x1_stored[r], 16 * TT // RING)

            def expert(s, par, shared):
                if inside(s, 0):
                    if isinstance(s, int) and s == TT:
                        sp.wait_ge(scattered, 16 * TT)
                    wait(sp, fx_turned, s - 1)
                    sp.dma_start(f_x[par], rows_in[bass.ds(s * P, P)]).then_inc(fx_loaded[par], 16)
                if inside(s, DOWN_LAG + 1):
                    t = s - DOWN_LAG - 1
                    sp.wait_ge(y_copied, t + 1)
                    sp.dma_start(rows_out[bass.ds(t * P, P)], f_y[1 - par]).then_inc(y_stored[1 - par], 16)

            ffn_steps(sp, expert, DOWN_LAG + 1)

            sp.wait_ge(h_turned, FT)

            def final(T, r, i):
                wait(sp, shared_added, T - RING + 1)
                sp.dma_start(x_res[r], rows_out[bass.ds(T * P, P)]).then_inc(ysh_in[r], 16)

            def final_store(T, r, i):
                sp.wait_ge(fin_made, T + 1)
                sp.dma_start(out[bass.ds(T * P, P)], x1[r]).then_inc(out_stored[r], 16)

            for r in range(RING):
                final(r, r, 0)
            with sp.Fori(1, TT // RING) as i:
                for r in range(RING):
                    final_store(RING * (i - 1) + r, r, i - 1)
                    final(RING * i + r, r, i)
            for r in range(RING):
                final_store(TT - RING + r, r, TT // RING - 1)
            for r in range(RING):
                sp.wait_ge(out_stored[r], 16 * TT // RING)

        @block.gpsimd
        def _(pool):
            pool.memset(zeros[:], 0.0).then_inc(pool_step, 1)
            pool.memset(ones[:], 1.0).then_inc(pool_step, 1)
            pool.memset(ones_bf[:], 1.0).then_inc(pool_step, 1)
            pool.memset(m_parts[:], 0.0).then_inc(pool_step, 1)
            pool.memset(eps[:], EPS).then_inc(pool_step, 1)
            pool.wait_ge(pool_step, 5)
            z = zeros[:, 0:P]
            for dst in (ident, ident_bf):
                pool.affine_select(dst[:], z, [[-1, P]], ALU.not_equal, 1.0, 0, 1).then_inc(consts_made, 1)
            pool.affine_select(mask_q[:], z, [[-1, P]], ALU.is_ge, MASKED, 0, 1).then_inc(consts_made, 1)
            pool.affine_select(mask_k[:], z, [[1, P]], ALU.is_ge, MASKED, 0, -1).then_inc(consts_made, 1)
            pool.affine_select(before[:], ones[:], [[1, P]], ALU.is_gt, 0.0, 0, -1).then_inc(consts_made, 1)

            def middle(b):
                for m in range(4):
                    pool.wait_ge(rest_made, 4 * b + m + 1)
                    pool.tensor_tensor(parts[m % 2][:, 1], rest[m % 2], zeros[:, 0:1].broadcast_to([P, S]),
                                       ALU.add).then_inc(mid_made, 1)

            with pool.Fori(0, B) as b:
                middle(b)


            def attend(b):
                for q in range(NQ):
                    g = NQ * b + q
                    wait(pool, pv_done, NT * (g - 1) + 2 if not isinstance(g, int) or g > 1 else 0)
                    pool.wait_ge(v_kept, 2 * B)
                    pool.tensor_copy(v_ext[q % 2][:, :, :, 0:DH],
                                     v_all[:, bass.ds(b, 1), :, q * QH * DH:(q + 1) * QH * DH]
                                     .rearrange("p o n (h d) -> p (o n) h d", h=QH)).then_inc(v_ready, 1)
                    pool.wait_ge(max_found, U * (g + 1))
                    wait(pool, m_turned, g)
                    n = QH * NT
                    nm = negmax[q % 2]
                    none = zeros[:, 0:n]
                    pool.tensor_tensor(m_parts[:, 0:n], nm[:], none, ALU.add).then_inc(m_step, 1)
                    pool.wait_ge(m_step, 3 * g + 1)
                    pool.tensor_tensor(m_rest[:], nm[:], m_parts[:, 0:n], ALU.subtract).then_inc(m_step, 1)
                    pool.wait_ge(m_step, 3 * g + 2)
                    pool.tensor_tensor(m_parts[:, n:2 * n], m_rest[:], none, ALU.add).then_inc(m_step, 1)
                    pool.wait_ge(m_step, 3 * g + 3)
                    pool.tensor_tensor(m_parts[:, 2 * n:3 * n], m_rest[:], m_parts[:, n:2 * n],
                                       ALU.subtract).then_inc(m_split, 1)

            attend(0)
            with pool.Fori(1, B) as b:
                attend(b)

            pool.wait_ge(att_kept, QUADS)

            def residual(at):
                kept, new = at(STORE_LAG), at(0)
                if kept:
                    pool.wait_ge(x1_made, kept[0] + 1)
                if new:
                    T, n, b = new
                    r = n % RING
                    wait(pool, att_turned, T - RING + 1)
                    wait(pool, sum_made, T - RING + 1)
                    pool.wait_ge(x_res_in[r], 16 * (b * (CT // RING) + n // RING + 1))
                    pool.tensor_tensor(xb[r], x_res[r], bo[:], ALU.add).then_inc(xb_made, 1)
                    pool.tensor_copy(att_in[r], res[:, bass.ds(T, 1)].rearrange("p o c -> p (o c)")).then_inc(att_staged, 1)
                if kept:
                    T, n, _ = kept
                    pool.tensor_copy(res[:, bass.ds(T, 1)].rearrange("p o c -> p (o c)"), x1[n % RING]).then_inc(x1_kept, 1)

            tile_rounds(pool, residual)

            pool.iota(route[3], [[0, TT], [-1, E]], E + 1, 0, allow_small_or_imprecise_dtypes=True).then_inc(iotas_made, 1)
            pool.iota(step128, [[0, E], [P, TT]], 0, 0, allow_small_or_imprecise_dtypes=True).then_inc(iotas_made, 1)
            pool.iota(tile_no, [[1, RT], [0, E]], 0, 0, allow_small_or_imprecise_dtypes=True).then_inc(iotas_made, 1)
            pool.wait_ge(zero_rows, 16)
            pool.wait_ge(routed, 1)
            pool.wait_ge(x1_kept, TT)
            for T in range(TT):
                pool.indirect_dma_start(rows_in, bass.IndirectOffsetOnAxis(ap=pos[:, T:T + 1], axis=0),
                                        res[:, T], None).then_inc(scattered, 16)

            for i in range(2):
                pool.wait_ge(y_stored[i], 16 * ((FT + 1 - i) // 2))
            for T in range(TT):
                wait(pool, gathered[T % RING], 16 * (T // RING))
                pool.indirect_dma_start(y_own[:, T], None, rows_out,
                                        bass.IndirectOffsetOnAxis(ap=pos[:, T:T + 1], axis=0)
                                        ).then_inc(gathered[T % RING], 16)

        @block.scalar
        def _(act):
            for e in range(EARLY):
                act.dma_start(weights[:, e * SLOT:(e + 1) * SLOT], w_sets[e]).then_inc(w_loaded[0], 16)
            act.sem_inc(exped, 2)
            act.sem_inc(o_copied, 1)
            act.wait_ge(consts_in, 16 * 6)

            def project(i, par):
                b = 2 * i + par
                act.wait_ge(x_turned, b + 1)
                wait(act, v_projected, b - 1)
                for k in range(KD):
                    act.activation(xT[par][:, k], ps[:, k], ACT.Copy).then_inc(xT_copied, 1)
                for m in range(4):
                    n = 4 * b + m
                    act.wait_ge(qk_projected, n + 1)
                    wait(act, rest_made, n - 1)
                    act.activation(qk32[m % 2], ps[:, 2 + m], ACT.Identity, bias=bqk[:, m:m + 1]).then_inc(qk_read, 1)
                    if not isinstance(b, int) or n >= 2:
                        wait(act, parts_stored[m % 2], 16 * (2 * b + m // 2))
                    act.activation(parts[m % 2][:, 0], ps[:, 2 + m], ACT.Identity,
                                   bias=bqk[:, m:m + 1]).then_inc(qk_read, 1)

            project(0, 0)
            project(0, 1)
            with act.Fori(1, B // 2) as i:
                project(i, 0)
                project(i, 1)

            def step(b, s):
                if (t := item(b, s, O_COPY)) and t[1] % U == 0:
                    g = NQ * t[0] + t[1] // U
                    act.wait_ge(pv_done, NT * (g + 1) + 2)
                    act.wait_ge(o_turned, g + 1)
                    act.activation(o_sb, ps[:, 6], ACT.Copy).then_inc(o_copied, 1)
                if (t := item(b, s, S_LAG)):
                    g, u = NQ * t[0] + t[1] // U, t[1] % U
                    j, pair = u // 2, u % 2
                    act.wait_ge(scored, U * g + u + 1)
                    act.wait_ge(pv_done, NT * g + j + 1)
                    n = S - j * P
                    act.activation(probs[:, j % 2, 2 * pair:2 * pair + 2, 0:n],
                                   ps[:, 2 + 2 * (u % 2):4 + 2 * (u % 2), 0:n], ACT.Exp, scale=SCALE).then_inc(exped, 1)
                if (t := item(b, s, M_TURN)) and t[1] % U == 0:
                    g = NQ * t[0] + t[1] // U
                    act.wait_ge(m_turned, g + 1)
                    wait(act, m_placed, 16 * g)
                    n = 3 * QH * NT
                    act.activation(m_rows[:], ps[0:n, 7, 0:P // 2].bitcast(BF16), ACT.Copy).then_inc(m_copied, 1)

            rounds(act, step)

            def residual(at):
                if t := at(0):
                    T, n, _ = t
                    act.wait_ge(att_turned, T + 1)
                    act.activation(attT[n % RING], ps[:, n % 2, 0:D].rearrange("p (k n) -> p k n", k=KD), ACT.Copy
                                   ).then_inc(attT_copied, 1)
                if t := at(NORM_LAG):
                    T, n, _ = t
                    act.wait_ge(var_made, T + 1)
                    act.activation(std[n % RING][:], stats[n % RING][:, 7:8], ACT.Sqrt, bias=eps[:]).then_inc(std_made, 1)
                if t := at(X1_LAG):
                    T, n, _ = t
                    act.wait_ge(x1_turned, T + 1)
                    act.activation(x1T[n % RING], ps[:, 4 + n % 2, 0:D].rearrange("p (k n) -> p k n", k=KD), ACT.Copy
                                   ).then_inc(x1T_copied, 1)

            tile_rounds(act, residual)

            act.wait_ge(logits_clipped, 1)
            act.activation(route[2], route[1], ACT.Sigmoid).then_inc(probs_made, 1)

            act.wait_ge(routed, 1)
            for T in range(RING):
                act.wait_ge(x1_stored[T], 16 * TT // RING)
            late = weights[:, EARLY * SLOT:].rearrange("p (e w) -> p e w", e=NW - EARLY)
            for e in range(EARLY, NW):
                act.dma_start(late[:, e - EARLY], w_sets[e]).then_inc(w_loaded[1], 16)

            def expert(s, par, shared):
                if inside(s, 0):
                    act.wait_ge(fx_turned, s + 1)
                    act.activation(f_xT[par], ps[:, 0, 0:D].rearrange("p (k n) -> p k n", k=KD), ACT.Copy
                                   ).then_inc(fxT_copied, 1)
                if inside(s, DOWN_LAG):
                    t = s - DOWN_LAG
                    act.wait_ge(h_turned, t + 1)
                    wait(act, y_made, t - 1)
                    act.activation(f_hT[par][:, 0:4], ps[:, 5].rearrange("p (k n) -> p k n", k=4), ACT.Copy
                                   ).then_inc(hT_copied_a, 1)
                if inside(s, UP_LAG):
                    t = s - UP_LAG
                    act.wait_ge(gate_up, t + 1)
                    wait(act, h_made, t)
                    act.activation(f_s.rearrange("p (a n) -> p a n", a=2), ps[:, 1:3, 0:PIECE], ACT.Silu).then_inc(silu_made, 1)
                if inside(s, DOWN_LAG):
                    t = s - DOWN_LAG
                    act.wait_ge(y_made, t + 1)
                    if not isinstance(s, int):
                        act.wait_ge(y_stored[par], 8 * (t - par))
                    elif t >= 2:
                        act.wait_ge(y_stored[par], 16 * (t // 2))
                    act.activation(f_y[par], ps[:, 7, 0:D], ACT.Copy).then_inc(y_copied, 1)

            ffn_steps(act, expert, DOWN_LAG)

            def final(T, r, i):
                act.wait_ge(var_made, TT + T + 1)
                act.activation(std[r][:], stats[r][:, 7:8], ACT.Sqrt, bias=eps[:]).then_inc(std_made, 1)

            final_rounds(act, final)

        @block.vector
        def _(v):
            v.wait_ge(consts_in, 16 * 6)

            def project(b):
                for m in range(4):
                    n = 4 * b + m
                    v.wait_ge(qk_read, 2 * (n + 1))
                    wait(v, low_made, n - 1)
                    v.tensor_tensor(rest[m % 2], qk32[m % 2], parts[m % 2][:, 0], ALU.subtract).then_inc(rest_made, 1)
                    v.wait_ge(mid_made, n + 1)
                    v.tensor_tensor(parts[m % 2][:, 2], rest[m % 2], parts[m % 2][:, 1], ALU.subtract
                                    ).then_inc(low_made, 1)
                v.wait_ge(v_projected, b + 1)
                dst = v_all[:, bass.ds(b, 1)].rearrange("p o (a n) c -> p (o a) n c", a=2)
                for a in range(2):
                    v.tensor_tensor(dst[:, a], ps[:, 6 + a].rearrange("p (n c) -> p n c", n=2),
                                    bv[:].unsqueeze(1).broadcast_to([P, 2, D]), ALU.add).then_inc(v_kept, 1)

            project(0)
            with v.Fori(1, B) as b:
                project(b)

            for i in range(2):
                v.wait_ge(parts_stored[i], 16 * 2 * B)
            v.wait_ge(v_projected, B)
            for q in range(NQ):
                v.memset(k_st[q][SR:SM], 1.0).then_inc(ones_rows, 1)
            for i in range(2):
                v.memset(v_ext[i][:, :, :, DH:2 * DH], 1.0).then_inc(ones_rows, 1)

            def step(b, s):
                if (t := item(b, s, 0)):
                    g, u = NQ * t[0] + t[1] // U, t[1] % U
                    i, pair = u // 2, u % 2
                    q = t[1] // U
                    v.wait_ge(max_scored, U * g + u + 1)
                    if u == 0:
                        wait(v, m_split, g - 1)
                    nm = negmax[q % 2][:].rearrange("p (h t) -> p h t", h=QH)
                    v.tensor_reduce(nm[:, 2 * pair:2 * pair + 2, i:i + 1], ps[:, 0:2, 0:(i + 1) * P], AX_X, ALU.max,
                                    negate=True).then_inc(max_found, 1)
                if (t := item(b, s, O_TURN + 1)) and t[1] % U == 0:
                    bb, q = t[0], t[1] // U
                    g = NQ * bb + q
                    v.wait_ge(o_turned, g + 2)
                    o = ps[:, 7].rearrange("p (t h d) -> p t h d", t=NT, h=QH)
                    v.reciprocal(rden[:].rearrange("p (t h) -> p t h", t=NT), o[:, :, :, DH]).then_inc(rden_made, 1)
                    v.wait_ge(rden_made, g + 1)
                    dst = res[:, bass.ds(NT * bb, NT), q * QH * DH:(q + 1) * QH * DH]
                    v.tensor_tensor(dst.rearrange("p t (h d) -> p t h d", h=QH), o[:, :, :, 0:DH],
                                    rden[:].rearrange("p (t h) -> p t h", t=NT).unsqueeze(3)
                                    .broadcast_to([P, NT, QH, DH]), ALU.mult).then_inc(att_kept, 1)

            rounds(v, step)

            v.wait_ge(consts_in, 16 * 6)

            def residual(at):
                new, old = at(PROJ_LAG), at(NORM_LAG)
                if old:
                    v.wait_ge(stats_made, old[0] + 1)
                if new:
                    T, n, _ = new
                    v.wait_ge(out_projected, T + 1)
                    v.wait_ge(xb_made, T + 1)
                    v.tensor_tensor(hid[n % RING], ps[:, 2 + n % 2, 0:D], xb[n % RING], ALU.add).then_inc(sum_made, 1)
                if old:
                    st = stats[old[1] % RING]
                    v.bn_aggr(st[:, 6:8], st[:, 0:6]).then_inc(var_made, 1)
                if new:
                    v.wait_ge(sum_made, T + 1)
                    v.bn_stats(stats[n % RING][:, 0:6], hid[n % RING]).then_inc(stats_made, 1)
                if old:
                    T, n, b = old
                    r = n % RING
                    v.wait_ge(std_made, T + 1)
                    v.reciprocal(rstd[r][:], std[r][:]).then_inc(rstd_made, 1)
                    v.wait_ge(rstd_made, T + 1)
                    wait(v, x1_turned, T - RING + 1)
                    wait(v, x1_kept, T - RING + 1)
                    wait(v, x1_stored[r], 16 * (b * (CT // RING) + n // RING))
                    v.tensor_scalar(x1[r], hid[r], stats[r][:, 6:7], rstd[r][:], ALU.subtract, ALU.mult
                                    ).then_inc(x1_made, 1)

            tile_rounds(v, residual)

            steps = [0]

            def link(ins):
                steps[0] += 1
                ins.then_inc(route_step, 1)
                v.wait_ge(route_step, steps[0])

            def over_e(c):
                return c.unsqueeze(2).broadcast_to([P, TT, E])

            def over_t(c):
                return c.unsqueeze(1).broadcast_to([P, TT, E])

            r0, r1, r2, desc, r4, onehot = route
            v.wait_ge(logits_made, TT)
            link(v.tensor_tensor(r0, ps[:, 6, 0:TE].rearrange("p (t e) -> p t e", t=TT), over_t(br[:]), ALU.add))
            v.tensor_scalar(r1, r0, 50.0, -50.0, ALU.min, ALU.max).then_inc(logits_clipped, 1)
            v.wait_ge(probs_made, 1)
            v.wait_ge(iotas_made, 3)
            link(v.tensor_reduce(col[0], r2, AX_X, ALU.max))
            link(v.tensor_tensor(r0, r2, over_e(col[0]), ALU.is_equal))
            link(v.tensor_tensor(r4, r0, desc, ALU.mult))
            link(v.tensor_reduce(col[1], r4, AX_X, ALU.max))
            link(v.tensor_tensor(onehot, r4, over_e(col[1]), ALU.is_equal))
            v.tensor_copy(onehot_bf, onehot.rearrange("p t e -> p (t e)")).then_inc(onehot_made, 1)
            link(v.tensor_scalar(col[2], col[0], 1.0 - 1e-8, 1e-8, ALU.min, ALU.max))
            link(v.tensor_scalar(col[1], col[2], 0.5, 1e-8, ALU.add, ALU.add))
            link(v.tensor_scalar(col[3], col[1], 2.0, 0.5, ALU.min, ALU.max))
            link(v.reciprocal(col[0], col[3]))
            link(v.tensor_scalar(share[:], col[0], 0.5, None, ALU.mult))
            link(v.tensor_tensor(gate[:], col[2], col[0], ALU.mult))
            v.wait_ge(counted, 1)
            count, tiles, end, start = [stats[i][:, 0:E] for i in range(4)]
            link(v.tensor_reduce(count, ps[:, 1, 0:TE].rearrange("p (t e) -> p e t", t=TT), AX_X, ALU.add))
            link(v.tensor_tensor(need, count.unsqueeze(2).broadcast_to([P, E, TT]), step128, ALU.is_gt))
            link(v.tensor_reduce(tiles, need, AX_X, ALU.add))
            link(v.tensor_copy(end, tiles))
            for e in range(1, E):
                link(v.tensor_tensor(end[:, e:e + 1], end[:, e - 1:e], tiles[:, e:e + 1], ALU.add))
            link(v.tensor_tensor(start, end, tiles, ALU.subtract))
            link(v.tensor_scalar(start, start, float(P), float(TOK), ALU.mult, ALU.add))
            link(v.tensor_tensor(r0, ps[:, 0, 0:TE].rearrange("p (t e) -> p t e", t=TT), over_t(start), ALU.add))
            link(v.tensor_tensor(r1, r0, onehot, ALU.mult))
            link(v.tensor_reduce(col[1], r1, AX_X, ALU.add))
            link(v.tensor_copy(pos[:], col[1]))
            link(v.tensor_tensor(tile_ge, tile_no, end[0:1].unsqueeze(1).broadcast_to([1, RT, E]), ALU.is_ge))
            link(v.tensor_reduce(tile_e[:], tile_ge[:, :, 0:E - 1], AX_X, ALU.add))
            v.tensor_scalar(tile_expert[:], tile_e[:], 1.0, None, ALU.add).then_inc(routed, 1)

            def expert(s, par, shared):
                if inside(s, DOWN_LAG):
                    t = s - DOWN_LAG
                    v.wait_ge(h_turned, t + 1)
                    wait(v, y_made, t - 1)
                    v.tensor_copy(f_hT[par][:, 4:KI], ps[:, 6, 0:(KI - 4) * P].rearrange("p (k n) -> p k n", k=KI - 4)
                                  ).then_inc(hT_copied_v, 1)
                if inside(s, UP_LAG):
                    t = s - UP_LAG
                    v.wait_ge(lin_up, t + 1)
                    v.wait_ge(silu_made, t + 1)
                    wait(v, h_turned, t - 1)
                    v.tensor_tensor(f_h[1 - par].rearrange("p (a n) -> p a n", a=2), f_s.rearrange("p (a n) -> p a n", a=2),
                                    ps[:, 3:5, 0:PIECE], ALU.mult).then_inc(h_made, 1)

            ffn_steps(v, expert, DOWN_LAG)

            def tile_of(a, T):
                return a[:, bass.ds(T, 1)].rearrange("p o c -> p (o c)")

            def normalize(T, r, i):
                v.wait_ge(std_made, TT + T + 1)
                v.reciprocal(rstd[r][:], std[r][:]).then_inc(rstd_made, 1)
                v.wait_ge(rstd_made, TT + T + 1)
                wait(v, out_stored[r], 16 * i)
                v.tensor_scalar(x1[r], hid[r], stats[r][:, 6:7], rstd[r][:], ALU.subtract, ALU.mult).then_inc(fin_made, 1)

            def final(T, r, i):
                last = (r - 1) % RING
                first = isinstance(T, int) and T == 0
                v.wait_ge(stats_made, TT + T)
                v.wait_ge(ysh_in[r], 16 * (i + 1))
                v.scalar_tensor_tensor(xb[r], x_res[r], share[:, bass.ds(T, 1)], tile_of(res, T), ALU.mult, ALU.add
                                       ).then_inc(shared_added, 1)
                if not first:
                    v.bn_aggr(stats[last][:, 6:8], stats[last][:, 0:6]).then_inc(var_made, 1)
                v.wait_ge(shared_added, T + 1)
                v.wait_ge(gathered[r], 16 * (i + 1))
                v.scalar_tensor_tensor(hid[r], tile_of(y_own, T), gate[:, bass.ds(T, 1)], xb[r], ALU.mult, ALU.add
                                       ).then_inc(sum_made, 1)
                v.wait_ge(sum_made, TT + T + 1)
                v.bn_stats(stats[r][:, 0:6], hid[r]).then_inc(stats_made, 1)
                if not first:
                    normalize(T - 1, last, i if r else i - 1)

            final_rounds(v, final)
            v.wait_ge(stats_made, 2 * TT)
            v.bn_aggr(stats[RING - 1][:, 6:8], stats[RING - 1][:, 0:6]).then_inc(var_made, 1)
            normalize(TT - 1, RING - 1, TT // RING - 1)

        @block.tensor
        def _(pe):
            pe.sem_inc(pv_done, 2)
            pe.sem_inc(o_turned, 1)
            pe.wait_ge(consts_made, 5)
            pe.wait_ge(consts_in, 16 * 6)
            pe.wait_ge(wqkv_in, 16)

            def project(i, par):
                b = 2 * i + par
                pe.wait_ge(x_loaded[par], 16 * (i + 1))
                wait(pe, xT_copied, KD * b)
                for k in range(KD):
                    for n in range(NT):
                        mm = pe.transpose(ps[:, k, n * P:(n + 1) * P], x_in[par][:, n, k * P:(k + 1) * P], ident[:])
                mm.then_inc(x_turned, 1)
                pe.wait_ge(xT_copied, KD * (b + 1))
                for m in range(4):
                    wait(pe, qk_read, 2 * (4 * b + m - 3))
                    for k in range(KD):
                        mm = pe.matmul(ps[:, 2 + m], wqkv[:, k, m * P:(m + 1) * P], xT[par][:, k],
                                       start=k == 0, stop=k == KD - 1)
                    mm.then_inc(qk_projected, 1)
                wait(pe, v_kept, 2 * b)
                for n in range(NT):
                    for k in range(KD):
                        mm = pe.matmul(ps[:, 6 + n // 2, (n % 2) * D:(n % 2 + 1) * D], xT[par][:, k, n * P:(n + 1) * P],
                                       wqkv[:, k, 2 * D:3 * D], start=k == 0, stop=k == KD - 1)
                mm.then_inc(v_projected, 1)

            project(0, 0)
            project(0, 1)
            with pe.Fori(1, B // 2) as i:
                project(i, 0)
                project(i, 1)

            pe.wait_ge(v_kept, 2 * B)
            pe.wait_ge(qk_read, 8 * B)
            pe.wait_ge(ones_rows, NQ + 2)

            def step(b, s):
                if (t := item(b, s, 0)):
                    g, q, u = NQ * t[0] + t[1] // U, t[1] // U, t[1] % U
                    i, pair = u // 2, u % 2
                    if u == 0:
                        pe.wait_ge(stack_loaded[q], 16 * 2 * NP_ * (t[0] + 1))
                    wait(pe, max_found, U * g + u)
                    n = (i + 1) * P
                    for a in range(2):
                        h = 2 * pair + a
                        pe.matmul(ps[:, a, 0:n], q_st[q][0:SR, h, i * P:n], k_st[q][0:SR, h, 0:n], start=True, stop=False)
                        mm = pe.matmul(ps[:, a, i * P:n], ident_bf[:], mask_q[:], start=False, stop=True)
                    mm.then_inc(max_scored, 1)
                if (t := item(b, s, S_LAG)):
                    g, q, u = NQ * t[0] + t[1] // U, t[1] // U, t[1] % U
                    j, pair = u // 2, u % 2
                    if u == 0:
                        pe.wait_ge(m_placed, 16 * (g + 1))
                    pe.wait_ge(exped, U * g + u + 1)
                    n = S - j * P
                    for a in range(2):
                        h = 2 * pair + a
                        dst = ps[:, 2 + 2 * (u % 2) + a]
                        pe.matmul(dst[:, 0:n], k_st[q][0:SM, h, j * P:(j + 1) * P], q_st[q][0:SM, h, j * P:S],
                                  start=True, stop=False)
                        mm = pe.matmul(dst[:, 0:P], ident_bf[:], mask_k[:], start=False, stop=True)
                    mm.then_inc(scored, 1)
                if (t := item(b, s, PV_LAG)) and t[1] % 2 == 0:
                    g, q, j = NQ * t[0] + t[1] // U, t[1] // U, t[1] % U // 2
                    pe.wait_ge(exped, U * g + 2 * j + 4)
                    if j == 0:
                        pe.wait_ge(v_ready, g + 1)
                        pe.wait_ge(o_copied, g + 1)
                    for h in range(QH):
                        mm = pe.matmul(ps[32 * h:32 * h + 32, 6, j * P:S], v_ext[q % 2][:, j, h],
                                       probs[:, j % 2, h, 0:S - j * P], start=j == 0, stop=j == NT - 1)
                    mm.then_inc(pv_done, 1)
                if (t := item(b, s, M_TURN)) and t[1] % U == 0:
                    g = NQ * t[0] + t[1] // U
                    pe.wait_ge(m_split, g + 1)
                    wait(pe, att_kept, g - 1)
                    pe.transpose(ps[:, 7, 0:P // 2].bitcast(BF16), m_parts[:], ident_bf[:]).then_inc(m_turned, 1)
                if (t := item(b, s, O_TURN)) and t[1] % U == 0:
                    g = NQ * t[0] + t[1] // U
                    pe.wait_ge(o_copied, g + 2)
                    wait(pe, att_kept, g)
                    pe.wait_ge(m_copied, min(g + 2, QUADS) if isinstance(g, int) else g + 2)
                    for n in range(NT):
                        mm = pe.transpose(ps[:, 7, n * P:(n + 1) * P], o_sb[:, n * P:(n + 1) * P], ident[:])
                    mm.then_inc(o_turned, 1)

            rounds(pe, step)

            pe.wait_ge(att_kept, QUADS)

            def residual(at):
                if t := at(0):
                    T, n, _ = t
                    pe.wait_ge(att_staged, T + 1)
                    wait(pe, attT_copied, T - 1)
                    for k in range(KD):
                        mm = pe.transpose(ps[:, n % 2, k * P:(k + 1) * P], att_in[n % RING][:, k * P:(k + 1) * P], ident[:])
                    mm.then_inc(att_turned, 1)
                if t := at(PROJ_LAG):
                    T, n, _ = t
                    pe.wait_ge(attT_copied, T + 1)
                    wait(pe, sum_made, T - 1)
                    for k in range(KD):
                        mm = pe.matmul(ps[:, 2 + n % 2, 0:D], attT[n % RING][:, k], wo[:, k], start=k == 0, stop=k == KD - 1)
                    mm.then_inc(out_projected, 1)
                if t := at(X1_LAG):
                    T, n, _ = t
                    pe.wait_ge(x1_made, T + 1)
                    wait(pe, x1T_copied, T - 1)
                    for k in range(KD):
                        mm = pe.transpose(ps[:, 4 + n % 2, k * P:(k + 1) * P], x1[n % RING][:, k * P:(k + 1) * P], ident[:])
                    mm.then_inc(x1_turned, 1)
                if t := at(LOGIT_LAG):
                    T, n, _ = t
                    pe.wait_ge(x1T_copied, T + 1)
                    for k in range(KD):
                        mm = pe.matmul(ps[:, 6, bass.ds(T * E, E)], x1T[n % RING][:, k], wr[:, k], start=k == 0, stop=k == KD - 1)
                    mm.then_inc(logits_made, 1)

            tile_rounds(pe, residual)

            def rank_tokens():
                pe.wait_ge(onehot_made, 1)
                pe.matmul(ps[:, 0, 0:TE], before[:], onehot_bf, start=True, stop=False)
                for T in range(TT - 1):
                    left = TT - 1 - T
                    pe.matmul(ps[:, 0, (T + 1) * E:TE].rearrange("p (t e) -> p t e", t=left), ones_bf[:],
                              onehot_bf[:, T * E:(T + 1) * E].unsqueeze(1).broadcast_to([P, left, E]),
                              start=False, stop=T == TT - 2)
                pe.matmul(ps[:, 1, 0:TE], ones_bf[:], onehot_bf, start=True, stop=True).then_inc(counted, 1)

            rank_tokens()
            pe.wait_ge(routed, 1)

            pe.wait_ge(w_loaded[0], 16 * EARLY)

            def expert(s, par, shared):
                if isinstance(s, int) and s == TT:
                    pe.wait_ge(w_loaded[1], 16 * (NW - EARLY))
                if inside(s, 0):
                    pe.wait_ge(fx_loaded[par], 8 * (s - par) + 16)
                    wait(pe, fxT_copied, s)
                    for k in range(KD):
                        mm = pe.transpose(ps[:, 0, k * P:(k + 1) * P], f_x[par][:, k * P:(k + 1) * P], ident[:])
                    mm.then_inc(fx_turned, 1)
                if inside(s, DOWN_LAG):
                    t = s - DOWN_LAG
                    pe.wait_ge(h_made, t + 1)
                    wait(pe, hT_copied_a, t)
                    wait(pe, hT_copied_v, t)
                    for k in range(KI):
                        n = P if k < KI - 1 else LAST
                        mm = pe.transpose(ps[0:n, 5 + k // 4, k % 4 * P:(k % 4 + 1) * P], f_h[par][:, k * P:k * P + n], ident[:])
                    mm.then_inc(h_turned, 1)
                if inside(s, UP_LAG):
                    t = s - UP_LAG
                    at = 0
                    if not shared(UP_LAG):
                        at = SLOT * pe.value_load(tile_expert[0:1, bass.ds(t - TT, 1)], min_val=1, max_val=E)
                    pe.wait_ge(fxT_copied, t + 1)
                    for half, bank, read, made in ((0, 1, silu_made, gate_up), (1, 3, h_made, lin_up)):
                        wait(pe, read, t)
                        for k in range(KD):
                            for a in range(2):
                                mm = pe.matmul(ps[:, bank + a, 0:PIECE], f_xT[1 - par][:, k],
                                               weights[:, bass.ds(at + k * UP + half * I + a * PIECE, PIECE)],
                                               start=k == 0, stop=k == KD - 1)
                        mm.then_inc(made, 1)
                if inside(s, DOWN_LAG):
                    t = s - DOWN_LAG
                    at = 0
                    if not shared(DOWN_LAG):
                        at = SLOT * pe.value_load(tile_expert[0:1, bass.ds(t - TT, 1)], min_val=1, max_val=E)
                    pe.wait_ge(hT_copied_a, t + 1)
                    pe.wait_ge(hT_copied_v, t + 1)
                    wait(pe, y_copied, t)
                    for k in range(KI):
                        n = P if k < KI - 1 else LAST
                        mm = pe.matmul(ps[:, 7, 0:D], f_hT[par][0:n, k], weights[0:n, bass.ds(at + UPW + k * D, D)],
                                       start=k == 0, stop=k == KI - 1)
                    mm.then_inc(y_made, 1)

            ffn_steps(pe, expert, DOWN_LAG)


def kernel(**inputs):
    import numpy as np
    import concourse.bacc as bacc
    from concourse import mybir as mb
    from concourse.bass_utils import run_bass_kernel_spmd

    a = {k.replace("L0_", ""): np.asarray(t) for k, t in inputs.items()}

    def by_rows(w):
        return w.reshape(*w.shape[:-2], -1, P, w.shape[-1]).swapaxes(-3, -2)

    def on_all(t):
        return np.broadcast_to(t, (P, t.size))

    sets = {}
    for n in (1, 2, 3):
        w = np.concatenate([a[f"ffn_sw{n}"][None], a[f"ffn_ew{n}"]])
        sets[n] = w.transpose(0, 2, 1)
    up = by_rows(np.concatenate([sets[1], sets[3]], axis=2)).reshape(NW, P, UPW)
    down = np.zeros((NW, KI * P, D), np.float32)
    down[:, :I] = sets[2]
    down = by_rows(down).reshape(NW, P, DNW)
    laid = {
        "x": a["attn_x"].reshape(TT, P, D),
        "w_qkv": by_rows(np.concatenate([a["attn_w_q"], a["attn_w_k"], a["attn_w_v"]], axis=1)),
        "b_qk": np.concatenate([a["attn_b_q"], a["attn_b_k"]]).reshape(4, P).T,
        "b_v": on_all(a["attn_b_v"]),
        "w_o": by_rows(a["attn_w_o"]),
        "b_o": on_all(a["attn_b_o"]),
        "w_r": by_rows(a["ffn_router_w"].T),
        "b_r": on_all(a["ffn_routing_bias"]),
        "w_sets": np.concatenate([up, down], axis=2),
    }
    nc = bacc.Bacc("TRN2", target_bir_lowering=False, num_devices=1)
    arrays, args = {}, {}
    for name, t in laid.items():
        arrays[f"in_{name}"] = np.ascontiguousarray(t)
        args[name] = nc.dram_tensor(f"in_{name}", t.shape, mb.dt.float32, kind="ExternalInput").ap()
    out = nc.dram_tensor("out_rows", (TOK, D), mb.dt.float32, kind="ExternalOutput").ap()
    block_kernel(nc, **args, out=out)
    r = run_bass_kernel_spmd(nc, [arrays], core_ids=[0])
    return r.results[0]["out_rows"].reshape(B, S, D)
```

```python
from contextlib import ExitStack

import concourse.bass as bass
from concourse import mybir

ALU = mybir.AluOpType
ACT = mybir.ActivationFunctionType
AX_X = mybir.AxisListType.X
F32 = mybir.dt.float32
F32R = mybir.dt.float32r
BF16 = mybir.dt.bfloat16
I32 = mybir.dt.int32
U32 = mybir.dt.uint32

P = 128
B, S, D = 8, 512, 256
H, DH = 16, 16
TOK = B * S
TT = TOK // P
NT = S // P
KD = D // P
QH = 4
NQ = H // QH
QUADS = B * NQ
I, E = 704, 7
NW = E + 1
UP = 2 * I
KI = -(-I // P)
LAST = I - (KI - 1) * P
UPW, DNW = KD * UP, KI * D
SLOT = UPW + DNW
PIECE = I // 2
RT = TT + E
SORTED = RT * P
RW = D + 2
SCALE = 0.25
EPS = 1e-5
MASKED = -1e30
K_PARTS = (0, 0, 1, 1, 0, 2)
Q_PARTS = (0, 1, 0, 1, 2, 0)
NP_ = len(K_PARTS)
SR = NP_ * DH
SM = SR + 3


def wait(eng, sem, count):
    if not isinstance(count, int) or count > 0:
        eng.wait_ge(sem, count)


def block_kernel(nc, x, w_qkv, b_qk, b_v, w_o, b_o, w_r, b_r, w_sets, out):
    with ExitStack() as ctx:
        def sb(name, shape, dt=F32):
            return ctx.enter_context(nc.sbuf_tensor(name, shape, dt))

        def sem(name):
            return ctx.enter_context(nc.semaphore(name))

        qk_parts = nc.dram_tensor("qk_parts", [2, 3, QUADS * QH * DH, S], BF16, kind="Internal").ap()
        rows_in = nc.dram_tensor("rows_in", [TOK + SORTED, D], F32, kind="Internal").ap()
        rows_rest = nc.dram_tensor("rows_rest", [SORTED, RW], F32, kind="Internal").ap()

        arena_at = -(-nc.sbuf_base // 32) * 32
        arena = sb("arena", [P, 8 * SLOT + 5632])
        WBUF = 4 * SLOT
        RAW, SCRATCH, WORK = 2 * SLOT, 4 * SLOT, 8 * SLOT

        def placed(name, words, at, dt=F32R):
            return nc.alloc_sbuf_tensor_at(name, [P, words], dt, offset=arena_at + 4 * at)

        w_split = placed("w_split", WBUF + 2 * SLOT, 0)
        raw = [placed(f"raw{i}", SLOT, RAW + i * SLOT, F32)[:] for i in range(2)]

        place = [0]

        def carve(words):
            at = place[0]
            place[0] += words
            assert at >= WORK or place[0] <= WORK
            assert place[0] <= WORK + 5632
            return arena[:, at:at + words]

        def carve_r(name, words):
            carve(words)
            return placed(name, words, place[0] - words)

        place[0] = SCRATCH
        v_all = carve(B * NT * D).rearrange("p (b n c) -> p b n c", b=B, n=NT)
        shared_at = place[0]
        x_in = [carve(NT * D).rearrange("p (n c) -> p n c", n=NT) for _ in range(2)]
        xT_hi = [carve_r(f"xT_hi{i}", KD * S)[:].rearrange("p (k n) -> p k n", k=KD) for i in range(2)]
        xT_lo = [carve_r(f"xT_lo{i}", KD * S)[:].rearrange("p (k n) -> p k n", k=KD) for i in range(2)]
        qk32 = [carve(S) for _ in range(2)]
        parts = [carve(3 * S // 2).bitcast(BF16).rearrange("p (t n) -> p t n", t=3) for _ in range(2)]
        place[0] = WORK
        wqkv = carve(KD * 3 * D)
        wqkv_hi = carve_r("wqkv_hi", KD * 3 * D)[:]
        wqkv_lo = carve_r("wqkv_lo", KD * 3 * D)[:]
        rest = [carve(S) for _ in range(2)]
        place[0] = shared_at
        q_st = [carve(QH * S // 2).bitcast(BF16).rearrange("p (h n) -> p h n", h=QH) for _ in range(NQ)]
        k_st = [carve(QH * S // 2).bitcast(BF16).rearrange("p (h n) -> p h n", h=QH) for _ in range(NQ)]
        v_ext = [carve(QH * S // 4).rearrange("p (n h d) -> p n h d", n=NT, h=QH) for _ in range(2)]
        place[0] = WORK
        probs = [carve(QH * (S - j * P)).rearrange("p (h n) -> p h n", h=QH) for j in range(NT)]
        o_sb = carve(S)
        RING = 8
        place[0] = SCRATCH
        att_in = [carve(D) for _ in range(RING)]
        attT = [carve(D).rearrange("p (k n) -> p k n", k=KD) for _ in range(RING)]
        x_res = [carve(D) for _ in range(RING)]
        xb = [carve(D) for _ in range(RING)]
        hid = [carve(D) for _ in range(RING)]
        x1 = [carve(D) for _ in range(RING)]
        x1T = [carve(D).rearrange("p (k n) -> p k n", k=KD) for _ in range(RING)]
        xh = [placed(f"xh{i}", D, 6 * SLOT + i * D)[:].rearrange("p (k n) -> p k n", k=KD) for i in range(2)]
        xl = [placed(f"xl{i}", D, 6 * SLOT + (2 + i) * D)[:].rearrange("p (k n) -> p k n", k=KD) for i in range(2)]
        hh = placed("hh", KI * P, 6 * SLOT + 4 * D)[:].rearrange("p (k n) -> p k n", k=KI)
        hl = placed("hl", KI * P, 6 * SLOT + 4 * D + KI * P)[:].rearrange("p (k n) -> p k n", k=KI)
        place[0] = 6 * SLOT + 4 * D + 2 * KI * P
        f_x = [carve(D) for _ in range(2)]
        f_s = carve(I)
        f_h = [carve(I) for _ in range(2)]
        f_rest = [carve(RW) for _ in range(2)]
        f_sum = [carve(D) for _ in range(2)]

        res = sb("res", [P, RT, RW])

        ident = sb("ident", [P, P])
        ident_bf = sb("ident_bf", [P, P], BF16)
        zeros = sb("zeros", [P, D])
        mask_q = sb("mask_q", [P, P], BF16)
        before = sb("before", [P, P], BF16)
        ones_bf = sb("ones_bf", [P, P], BF16)
        bqk = sb("bqk", [P, 4])
        template = sb("template", [P, RW])
        bv = sb("bv", [P, D])
        bo = sb("bo", [P, D])
        wo = sb("wo", [P, KD, D])
        wr = sb("wr", [P, KD, E])
        br = sb("br", [P, E])
        negmax = [sb(f"negmax{i}", [P, QH * NT]) for i in range(2)]
        idle = sb("idle", [P, 1])
        m_rest = sb("m_rest", [P, QH * NT])
        m_parts = sb("m_parts", [P, P], BF16)
        m_rows = sb("m_rows", [3 * QH * NT, P], BF16)
        rden = sb("rden", [P, NT * QH])
        stats = [sb(f"stats{i}", [P, 8]) for i in range(RING)]
        std = [sb(f"std{i}", [P, 1]) for i in range(RING)]
        eps = sb("eps", [P, 1])
        rstd = [sb(f"rstd{i}", [P, 1]) for i in range(RING)]
        TE = TT * E
        place[0] = SCRATCH + 7 * RING * D
        grid = lambda t: t.rearrange("p (t e) -> p t e", t=TT)
        route = [grid(carve(TT * E)) for _ in range(6)]
        onehot_bf = carve(TT * E // 2).bitcast(BF16)
        col = [carve(TT) for _ in range(4)]
        share = sb("share", [P, TT])
        pos = sb("pos", [P, TT], U32)
        std_all = sb("std_all", [P, RT])
        rstd_all = sb("rstd_all", [P, RT])
        ends = sb("ends", [1, E], I32)
        tile_par = sb("tile_par", [1, RT], I32)
        need = carve(E * TT).rearrange("p (e t) -> p e t", e=E)
        step128 = carve(E * TT).rearrange("p (e t) -> p e t", e=E)
        tiles_of = [sb(f"tiles_of{i}", [P, E]) for i in range(2)]
        tile_no = carve(RT * E)[0:1].rearrange("p (t e) -> p t e", t=RT)
        tile_ge = carve(RT * E)[0:1].rearrange("p (t e) -> p t e", t=RT)
        tile_e = sb("tile_e", [1, RT])
        tile_expert = sb("tile_expert", [1, RT], I32)

        ps = ctx.enter_context(nc.psum_tensor("ps", [P, 8, 512], F32))

        consts_in = sem("consts_in")
        wqkv_in = sem("wqkv_in")
        consts_made = sem("consts_made")
        pool_step = sem("pool_step")
        x_loaded = [sem(f"x_loaded{i}") for i in range(2)]
        x_turned = sem("x_turned")
        wqkv_split = sem("wqkv_split")
        xT_copied = sem("xT_copied")
        xT_low = sem("xT_low")
        qk_projected = sem("qk_projected")
        v_projected = sem("v_projected")
        qk_read = sem("qk_read")
        rest_made = sem("rest_made")
        mid_made = sem("mid_made")
        low_made = sem("low_made")
        v_kept = sem("v_kept")
        parts_stored = [sem(f"parts_stored{i}") for i in range(2)]
        stack_loaded = [sem(f"stack_loaded{i}") for i in range(NQ)]
        ones_rows = sem("ones_rows")
        max_scored = sem("max_scored")
        max_found = sem("max_found")
        m_step = sem("m_step")
        m_split = sem("m_split")
        m_turned = sem("m_turned")
        m_copied = sem("m_copied")
        m_placed = sem("m_placed")
        scored = sem("scored")
        exped = sem("exped")
        masked = sem("masked")
        v_ready = sem("v_ready")
        pv_done = sem("pv_done")
        o_copied = sem("o_copied")
        o_turned = sem("o_turned")
        rden_made = sem("rden_made")
        att_kept = sem("att_kept")
        raw_in = [sem(f"raw_in{i}") for i in range(2)]
        split_step = sem("split_step")
        split_done = sem("split_done")
        template_made = sem("template_made")
        zero_rows = sem("zero_rows")
        x_res_in = [sem(f"x_res_in{i}") for i in range(RING)]
        att_staged = sem("att_staged")
        xb_made = sem("xb_made")
        att_turned = sem("att_turned")
        attT_copied = sem("attT_copied")
        out_projected = sem("out_projected")
        sum_made = sem("sum_made")
        stats_made = sem("stats_made")
        var_made = sem("var_made")
        rstd_made = sem("rstd_made")
        std_made = sem("std_made")
        x1_made = sem("x1_made")
        x1_kept = sem("x1_kept")
        x1_stored = [sem(f"x1_stored{i}") for i in range(RING)]
        x1_turned = sem("x1_turned")
        x1T_copied = sem("x1T_copied")
        logits_made = sem("logits_made")
        iotas_made = sem("iotas_made")
        logits_clipped = sem("logits_clipped")
        probs_made = sem("probs_made")
        onehot_made = sem("onehot_made")
        counted = sem("counted")
        route_step = sem("route_step")
        routed = sem("routed")
        scattered = sem("scattered")
        fx_loaded = [sem(f"fx_loaded{i}") for i in range(2)]
        fx_turned = sem("fx_turned")
        fx_high = sem("fx_high")
        fx_low = sem("fx_low")
        gate_up = sem("gate_up")
        lin_up = sem("lin_up")
        silu_made = sem("silu_made")
        h_made = sem("h_made")
        h_turned = sem("h_turned")
        h_high = sem("h_high")
        h_low = sem("h_low")
        y_made = sem("y_made")
        y_read = sem("y_read")
        rest_scattered = sem("rest_scattered")
        f_rest_in = [sem(f"f_rest_in{i}") for i in range(2)]
        sum_stats = sem("sum_stats")
        sum_stats2 = sem("sum_var")
        sum_kept = sem("sum_kept")
        stds_made = sem("stds_made")
        rstds_made = sem("rstds_made")
        normed = sem("normed")
        out_scattered = sem("out_scattered")

        h_banks = ps[:, 5:7].rearrange("p a n -> p (a n)")[:, 0:KI * P].rearrange("p (k n) -> p k n", k=KI)
        qk_rows = QH * DH
        qk_store = qk_parts.rearrange("w t r n -> w r t n")

        block = ctx.enter_context(nc.Block())

        M_UNITS = [(i, h, n) for i in range(NT) for n in (2 if i < NT // 2 else 1,) for h in range(0, QH, n)]
        S_UNITS = [(j, h, n) for j in range(NT) for n in (1 if j < NT // 2 else 2,) for h in range(0, QH, n)]
        U = len(M_UNITS)
        SLOTS = 3
        STEPS = NQ * U
        assert STEPS % SLOTS == 0
        S_LAST = {max(u for u in range(U) if S_UNITS[u][0] == j): j for j in range(NT)}
        M_TURN, S_LAG, V_LAG = 17, 22, 16
        PV_LAG, O_COPY, O_TURN = S_LAG + 3, S_LAG + 15, S_LAG + 16

        def item(b, s, lag):
            d, n = divmod(s - lag, STEPS)
            if isinstance(b, int) and not 0 <= b + d < B:
                return None
            if lag == 0 and d < 0:
                return None
            return b + d, n

        CT = 8
        PROJ_LAG, NORM_LAG, STORE_LAG, X1_LAG, LOGIT_LAG, KEEP_LAG = 2, 3, 4, 5, 6, 7

        def tile_rounds(eng, body):
            def one(b):
                for s in range(CT):
                    def at(lag, b=b, s=s):
                        d, n = divmod(s - lag, CT)
                        if isinstance(b, int) and not 0 <= b + d < TT // CT:
                            return None
                        return (b + d) * CT + n, n, b + d
                    body(at)
            one(0)
            one(1)
            with eng.Fori(2, TT // CT) as b:
                one(b)
            one(TT // CT)

        FT = TT + RT
        UP_LAG, DOWN_LAG, SUM_LAG = 1, 2, 3
        STEADY = 4
        CHECKS = (14, 24, 32, RT)

        def ffn_steps(eng, body, check=None):
            def one(s, par, first):
                body(s, par, lambda lag: first - lag < TT)

            def straight(a, b):
                for s in range(a, b):
                    one(s, s % 2, s)

            def loop(a, b):
                kind = STEADY if b <= TT else TT + STEADY
                with eng.Fori(a // 2, b // 2) as i:
                    for par in range(2):
                        one(2 * i + par, par, kind + par)

            straight(0, STEADY)
            loop(STEADY, TT)
            straight(TT, TT + STEADY)
            at, done = TT + STEADY, 0
            for c in CHECKS[:-1]:
                end = TT + c + SUM_LAG + 1
                loop(at, end)
                if check:
                    check(done, c)
                at, done = end, c
            last = FT // 2 * 2
            loop(at, last)
            straight(last, FT + SUM_LAG + 1)
            if check:
                check(done, RT)

        def inside(s, lag):
            return not isinstance(s, int) or 0 <= s - lag < FT

        def rounds(eng, body):
            def one(b):
                for s in range(STEPS):
                    body(b, s)
            one(0)
            with eng.Fori(1, B) as b:
                one(b)
            one(B)

        @block.sync
        def _(sp):
            sp.dma_start(wqkv, w_qkv.rearrange("p k n -> p (k n)")).then_inc(wqkv_in, 16)

            def proj_batch(i, par):
                b = 2 * i + par
                wait(sp, x_turned, b - 1)
                sp.dma_start(x_in[par], x[bass.ds(b * NT, NT)].rearrange("n p c -> p n c")).then_inc(x_loaded[par], 16)

            def store_batch(b):
                for m in range(4):
                    sp.wait_ge(low_made, 4 * b + m + 1)
                    sp.dma_start(qk_store[m // 2, bass.ds((4 * b + 2 * (m % 2)) * qk_rows, P)],
                                 parts[m % 2]).then_inc(parts_stored[m % 2], 16)

            proj_batch(0, 0)
            for dst, src in ((bqk, b_qk), (bv, b_v), (bo, b_o), (br, b_r), (wo, w_o), (wr, w_r)):
                sp.dma_start(dst[:], src).then_inc(consts_in, 16)
            proj_batch(0, 1)
            store_batch(0)
            with sp.Fori(1, B // 2) as i:
                proj_batch(i, 0)
                store_batch(2 * i - 1)
                proj_batch(i, 1)
                store_batch(2 * i)
            store_batch(B - 1)

            def load_stack(b, q):
                wait(sp, scored, U * (NQ * b + q - NQ + 1))
                for t in range(NP_):
                    for side, st, which in ((0, q_st, Q_PARTS), (1, k_st, K_PARTS)):
                        src = qk_parts[side, which[t], bass.ds((NQ * b + q) * qk_rows, qk_rows)]
                        sp.dma_start(st[q][t * DH:(t + 1) * DH], src.rearrange("(h d) n -> d h n", h=QH)
                                     ).then_inc(stack_loaded[q], 16)

            def place_max(b, q):
                sp.wait_ge(m_copied, NQ * b + q + 1)
                sp.dma_start(q_st[q][SR:SM].rearrange("p h n -> p (h n)"), m_rows[:]).then_inc(m_placed, 16)

            for i in range(2):
                sp.wait_ge(parts_stored[i], 16 * 2 * B)
            sp.wait_ge(v_projected, B)
            load_stack(0, 0)
            load_stack(0, 1)
            sp.wait_ge(template_made, 2)
            for dst, w in ((rows_in[TOK:TOK + SORTED], D), (rows_rest, RW)):
                sp.dma_start(dst.rearrange("(t p) c -> p t c", p=P),
                             template[:, 0:w].unsqueeze(1).broadcast_to([P, RT, w])).then_inc(zero_rows, 16)

            def stacks(b):
                for q in range(NQ):
                    if q < 2:
                        load_stack(b, q + 2)
                    elif not (isinstance(b, int) and b == B - 1):
                        load_stack(b + 1, q - 2)
                    place_max(b, q)

            stacks(0)
            with sp.Fori(1, B - 1) as b:
                stacks(b)
            stacks(B - 1)
            sp.wait_ge(att_kept, QUADS)

            def residual(at):
                if t := at(0):
                    T, n, _ = t
                    wait(sp, xb_made, T - RING + 1)
                    sp.dma_start(x_res[n % RING], x[bass.ds(T, 1)].rearrange("o p c -> (o p) c")
                                 ).then_inc(x_res_in[n % RING], 16)
                if t := at(STORE_LAG):
                    T, n, _ = t
                    sp.wait_ge(x1_made, T + 1)
                    sp.dma_start(rows_in[bass.ds(T * P, P)], x1[n % RING]).then_inc(x1_stored[n % RING], 16)

            tile_rounds(sp, residual)

            for r in range(RING):
                sp.wait_ge(x1_stored[r], 16 * TT // RING)
            sp.wait_ge(x1_kept, TT)
            sp.wait_ge(x1_turned, TT)

            def expert(s, par, shared):
                if inside(s, 0):
                    if isinstance(s, int) and s == TT:
                        sp.wait_ge(scattered, 16 * TT)
                    wait(sp, fx_turned, s - 1)
                    sp.dma_start(f_x[par], rows_in[bass.ds(s * P, P)]).then_inc(fx_loaded[par], 16)
                if inside(s, DOWN_LAG) and not shared(DOWN_LAG):
                    t = s - DOWN_LAG
                    if isinstance(t, int) and t == TT:
                        sp.wait_ge(rest_scattered, 16 * TT)
                    wait(sp, sum_kept, t - TT - 1)
                    sp.dma_start(f_rest[par], rows_rest[bass.ds((t - TT) * P, P)]).then_inc(f_rest_in[par], 16)

            ffn_steps(sp, expert)
            sp.wait_ge(out_scattered, 16 * RT)

        @block.gpsimd
        def _(pool):
            pool.memset(zeros[:], 0.0).then_inc(pool_step, 1)
            pool.memset(ones_bf[:], 1.0).then_inc(pool_step, 1)
            pool.memset(m_parts[:], 0.0).then_inc(pool_step, 1)
            pool.memset(eps[:], EPS).then_inc(pool_step, 1)
            pool.memset(template[:], 0.0).then_inc(pool_step, 1)
            pool.wait_ge(pool_step, 5)
            z = zeros[:, 0:P]
            for dst in (ident, ident_bf):
                pool.affine_select(dst[:], z, [[-1, P]], ALU.not_equal, 1.0, 0, 1).then_inc(consts_made, 1)
            pool.wait_ge(wqkv_in, 16)
            pool.tensor_copy(wqkv_hi, wqkv).then_inc(wqkv_split, 1)
            pool.wait_ge(wqkv_split, 1)
            pool.tensor_tensor(wqkv_lo, wqkv, wqkv_hi.bitcast(F32), ALU.subtract).then_inc(wqkv_split, 1)
            pool.affine_select(mask_q[:], z, [[-1, P]], ALU.is_ge, MASKED, 0, 1).then_inc(consts_made, 1)
            pool.affine_select(before[:], ones_bf[:], [[1, P]], ALU.is_gt, 0.0, 0, -1).then_inc(consts_made, 1)
            pool.iota(template[:, D + 1:RW].bitcast(I32), [[0, 1]], 1 << 20, 0).then_inc(template_made, 1)
            pool.iota(res[:, 0:TT, D + 1:RW].bitcast(I32), [[P, TT], [0, 1]], 0, 1).then_inc(template_made, 1)

            def load_set(w):
                pool.dma_start(raw[w % 2], w_sets[w]).then_inc(raw_in[w % 2], 16)

            def split_set(w):
                at = w % 2 * WBUF
                pool.wait_ge(raw_in[w % 2], 16 * (w // 2 + 1))
                pool.tensor_copy(w_split[:, at:at + SLOT], raw[w % 2]).then_inc(split_step, 1)
                pool.wait_ge(split_step, w + 1)
                pool.tensor_tensor(w_split[:, at + SLOT:at + 2 * SLOT], raw[w % 2], w_split[:, at:at + SLOT].bitcast(F32),
                                   ALU.subtract).then_inc(split_done, 1)
                if w + 2 < NW:
                    pool.wait_ge(split_done, w + 1)
                    load_set(w + 2)

            for i in range(2):
                pool.wait_ge(x_loaded[i], 16)
            load_set(0)
            load_set(1)

            def middle(b):
                for m in range(4):
                    pool.wait_ge(rest_made, 4 * b + m + 1)
                    pool.tensor_tensor(parts[m % 2][:, 1], rest[m % 2], zeros[:, 0:1].broadcast_to([P, S]),
                                       ALU.add).then_inc(mid_made, 1)

            with pool.Fori(0, B) as b:
                middle(b)
            split_set(0)


            def attend(b, s):
                if (t := item(b, s, V_LAG)) and t[1] % U == 0:
                    g, q = NQ * t[0] + t[1] // U, t[1] // U
                    wait(pool, pv_done, NT * g if not isinstance(g, int) or g > 1 else 0)
                    pool.wait_ge(v_kept, 2 * B)
                    pool.tensor_copy(v_ext[q % 2][:, :, :, 0:DH],
                                     v_all[:, bass.ds(t[0], 1), :, q * QH * DH:(q + 1) * QH * DH]
                                     .rearrange("p o n (h d) -> p (o n) h d", h=QH)).then_inc(v_ready, 1)
                if (t := item(b, s, S_LAG)) and t[1] % U in S_LAST:
                    g, j = NQ * t[0] + t[1] // U, S_LAST[t[1] % U]
                    wait(pool, masked, NT * g + j)
                    pool.wait_ge(exped, U * g + t[1] % U + 1 + SLOTS)
                    pool.tensor_tensor(idle[:], zeros[:, 0:1], zeros[:, 0:1], ALU.add)
                    diagonal = probs[j][:, :, 0:P]
                    pool.affine_select(diagonal, diagonal, [[0, QH], [1, P]], ALU.is_ge, 0.0, 0, -1).then_inc(masked, 1)
                if (t := item(b, s, U - 1)) and t[1] % U == 0:
                    g, q = NQ * t[0] + t[1] // U, t[1] // U
                    pool.wait_ge(max_found, U * (g + 1))
                    wait(pool, m_turned, g)
                    n = QH * NT
                    nm = negmax[q % 2]
                    none = zeros[:, 0:n]
                    pool.tensor_tensor(m_parts[:, 0:n], nm[:], none, ALU.add).then_inc(m_step, 1)
                    pool.wait_ge(m_step, 3 * g + 1)
                    pool.tensor_tensor(m_rest[:], nm[:], m_parts[:, 0:n], ALU.subtract).then_inc(m_step, 1)
                    pool.wait_ge(m_step, 3 * g + 2)
                    pool.tensor_tensor(m_parts[:, n:2 * n], m_rest[:], none, ALU.add).then_inc(m_step, 1)
                    pool.wait_ge(m_step, 3 * g + 3)
                    pool.tensor_tensor(m_parts[:, 2 * n:3 * n], m_rest[:], m_parts[:, n:2 * n],
                                       ALU.subtract).then_inc(m_split, 1)

            rounds(pool, attend)

            pool.wait_ge(att_kept, QUADS)

            def residual(at):
                kept, new = at(KEEP_LAG), at(0)
                if kept:
                    pool.wait_ge(x1_made, kept[0] + 1)
                if new:
                    T, n, b = new
                    r = n % RING
                    wait(pool, att_turned, T - RING + 1)
                    wait(pool, sum_made, T - RING + 1)
                    pool.wait_ge(x_res_in[r], 16 * (b * (CT // RING) + n // RING + 1))
                    pool.tensor_tensor(xb[r], x_res[r], bo[:], ALU.add).then_inc(xb_made, 1)
                    pool.tensor_copy(att_in[r], res[:, bass.ds(T, 1), 0:D].rearrange("p o c -> p (o c)")).then_inc(att_staged, 1)
                if kept:
                    T, n, _ = kept
                    pool.tensor_copy(res[:, bass.ds(T, 1), 0:D].rearrange("p o c -> p (o c)"), x1[n % RING]).then_inc(x1_kept, 1)

            tile_rounds(pool, residual)

            pool.iota(route[3], [[0, TT], [-1, E]], E + 1, 0, allow_small_or_imprecise_dtypes=True).then_inc(iotas_made, 1)
            pool.iota(step128, [[0, E], [P, TT]], 0, 0, allow_small_or_imprecise_dtypes=True).then_inc(iotas_made, 1)
            pool.iota(tile_no, [[1, RT], [0, E]], 0, 0, allow_small_or_imprecise_dtypes=True).then_inc(iotas_made, 1)
            pool.wait_ge(routed, 1)
            for r in range(RING):
                pool.wait_ge(x1_stored[r], 16 * TT // RING)
            pool.wait_ge(x1_kept, TT)
            pool.wait_ge(zero_rows, 32)
            for T in range(TT):
                pool.indirect_dma_start(rows_in, bass.IndirectOffsetOnAxis(ap=pos[:, T:T + 1], axis=0),
                                        res[:, T, 0:D], None, element_offset=TOK * D).then_inc(scattered, 16)
            split_set(1)
            for T in range(TT):
                pool.wait_ge(y_read, T + 1)
                pool.indirect_dma_start(rows_rest, bass.IndirectOffsetOnAxis(ap=pos[:, T:T + 1], axis=0),
                                        res[:, T], None).then_inc(rest_scattered, 16)
            split_set(2)
            for w in range(3, NW):
                done = pool.value_load(ends[0:1, w - 3:w - 2], min_val=TT + 1, max_val=FT)
                pool.wait_ge(y_made, done)
                pool.tensor_tensor(idle[:], zeros[:, 0:1], zeros[:, 0:1], ALU.add)
                split_set(w)
            for t in range(RT):
                pool.wait_ge(normed, t + 1)
                pool.indirect_dma_start(out, bass.IndirectOffsetOnAxis(ap=res[:, t, D + 1:RW].bitcast(U32), axis=0),
                                        res[:, t, 0:D], None, bounds_check=TOK - 1, oob_is_err=False
                                        ).then_inc(out_scattered, 16)

        @block.scalar
        def _(act):
            act.sem_inc(exped, SLOTS)
            act.sem_inc(o_copied, 1)
            act.wait_ge(consts_in, 16 * 6)

            def project(i, par):
                b = 2 * i + par
                act.wait_ge(x_turned, b + 1)
                wait(act, v_projected, b - 1)
                for k in range(KD):
                    act.activation(xT_hi[par][:, k], ps[:, k], ACT.Copy).then_inc(xT_copied, 1)
                for m in range(4):
                    n = 4 * b + m
                    act.wait_ge(qk_projected, n + 1)
                    wait(act, rest_made, n - 1)
                    act.activation(qk32[m % 2], ps[:, 2 + m], ACT.Identity, bias=bqk[:, m:m + 1]).then_inc(qk_read, 1)
                    if not isinstance(b, int) or n >= 2:
                        wait(act, parts_stored[m % 2], 16 * (2 * b + m // 2))
                    act.activation(parts[m % 2][:, 0], ps[:, 2 + m], ACT.Identity,
                                   bias=bqk[:, m:m + 1]).then_inc(qk_read, 1)

            project(0, 0)
            project(0, 1)
            with act.Fori(1, B // 2) as i:
                project(i, 0)
                project(i, 1)

            def step(b, s):
                if (t := item(b, s, O_COPY)) and t[1] % U == 0:
                    g = NQ * t[0] + t[1] // U
                    act.wait_ge(pv_done, NT * (g + 2))
                    act.wait_ge(o_turned, g + 1)
                    act.activation(o_sb, ps[:, 6], ACT.Copy).then_inc(o_copied, 1)
                if (t := item(b, s, S_LAG)):
                    g, u = NQ * t[0] + t[1] // U, t[1] % U
                    j, h, n = S_UNITS[u]
                    w = S - j * P
                    act.wait_ge(scored, U * g + u + 1)
                    act.wait_ge(pv_done, NT * g + j + 1)
                    act.activation(probs[j][:, h:h + n], ps[:, 3 + t[1] % SLOTS, 0:n * w].rearrange("p (h n) -> p h n", h=n),
                                   ACT.Exp, scale=SCALE).then_inc(exped, 1)
                if (t := item(b, s, M_TURN)) and t[1] % U == 0:
                    g = NQ * t[0] + t[1] // U
                    act.wait_ge(m_turned, g + 1)
                    wait(act, m_placed, 16 * g)
                    n = 3 * QH * NT
                    act.activation(m_rows[:], ps[0:n, 7, 0:P // 2].bitcast(BF16), ACT.Copy).then_inc(m_copied, 1)

            rounds(act, step)

            def residual(at):
                if t := at(0):
                    T, n, _ = t
                    act.wait_ge(att_turned, T + 1)
                    act.activation(attT[n % RING], ps[:, n % 2, 0:D].rearrange("p (k n) -> p k n", k=KD), ACT.Copy
                                   ).then_inc(attT_copied, 1)
                if t := at(NORM_LAG):
                    T, n, _ = t
                    act.wait_ge(var_made, T + 1)
                    act.activation(std[n % RING][:], stats[n % RING][:, 7:8], ACT.Sqrt, bias=eps[:]).then_inc(std_made, 1)
                if t := at(X1_LAG):
                    T, n, _ = t
                    act.wait_ge(x1_turned, T + 1)
                    act.activation(x1T[n % RING], ps[:, 4 + n % 2, 0:D].rearrange("p (k n) -> p k n", k=KD), ACT.Copy
                                   ).then_inc(x1T_copied, 1)

            tile_rounds(act, residual)

            act.wait_ge(logits_clipped, 1)
            act.activation(route[2], route[1], ACT.Sigmoid).then_inc(probs_made, 1)

            def expert(s, par, shared):
                if inside(s, 0):
                    act.wait_ge(fx_turned, s + 1)
                    act.activation(xh[par], ps[:, 0, 0:D].rearrange("p (k n) -> p k n", k=KD), ACT.Copy
                                   ).then_inc(fx_high, 1)
                if inside(s, DOWN_LAG):
                    act.wait_ge(h_turned, s - DOWN_LAG + 1)
                    act.activation(hh, h_banks, ACT.Copy).then_inc(h_high, 1)
                if inside(s, UP_LAG):
                    t = s - UP_LAG
                    act.wait_ge(gate_up, t + 1)
                    wait(act, h_made, t)
                    act.activation(f_s.rearrange("p (a n) -> p a n", a=2), ps[:, 1:3, 0:PIECE], ACT.Silu).then_inc(silu_made, 1)

            def check(a, b):
                act.wait_ge(sum_kept, b)
                act.activation(std_all[:, a:b], res[:, a:b, D], ACT.Sqrt, bias=eps[:]).then_inc(stds_made, 1)

            ffn_steps(act, expert, check)

        @block.vector
        def _(v):
            v.wait_ge(consts_in, 16 * 6)

            def project(i, par):
                b = 2 * i + par
                for k in range(KD):
                    v.wait_ge(xT_copied, KD * b + k + 1)
                    v.tensor_tensor(xT_lo[par][:, k], ps[:, k], xT_hi[par][:, k].bitcast(F32), ALU.subtract
                                    ).then_inc(xT_low, 1)
                for m in range(4):
                    n = 4 * b + m
                    v.wait_ge(qk_read, 2 * (n + 1))
                    wait(v, low_made, n - 1)
                    v.tensor_tensor(rest[m % 2], qk32[m % 2], parts[m % 2][:, 0], ALU.subtract).then_inc(rest_made, 1)
                    v.wait_ge(mid_made, n + 1)
                    v.tensor_tensor(parts[m % 2][:, 2], rest[m % 2], parts[m % 2][:, 1], ALU.subtract
                                    ).then_inc(low_made, 1)
                v.wait_ge(v_projected, b + 1)
                dst = v_all[:, bass.ds(b, 1)].rearrange("p o (a n) c -> p (o a) n c", a=2)
                for a in range(2):
                    v.tensor_tensor(dst[:, a], ps[:, 6 + a].rearrange("p (n c) -> p n c", n=2),
                                    bv[:].unsqueeze(1).broadcast_to([P, 2, D]), ALU.add).then_inc(v_kept, 1)

            project(0, 0)
            project(0, 1)
            with v.Fori(1, B // 2) as i:
                project(i, 0)
                project(i, 1)

            for i in range(2):
                v.wait_ge(parts_stored[i], 16 * 2 * B)
            v.wait_ge(v_projected, B)
            for q in range(NQ):
                v.memset(k_st[q][SR:SM], 1.0).then_inc(ones_rows, 1)
            for i in range(2):
                v.memset(v_ext[i][:, :, :, DH:2 * DH], 1.0).then_inc(ones_rows, 1)

            def step(b, s):
                if (t := item(b, s, 0)):
                    g, q, u = NQ * t[0] + t[1] // U, t[1] // U, t[1] % U
                    i, h, n = M_UNITS[u]
                    w = (i + 1) * P
                    v.wait_ge(max_scored, U * g + u + 1)
                    if u == 0:
                        wait(v, m_split, g - 1)
                    nm = negmax[q % 2][:].rearrange("p (h t) -> p h t", h=QH)
                    v.tensor_reduce(nm[:, h:h + n, i:i + 1], ps[:, t[1] % SLOTS, 0:n * w].rearrange("p (h n) -> p h n", h=n),
                                    AX_X, ALU.max, negate=True).then_inc(max_found, 1)
                if (t := item(b, s, O_TURN + 1)) and t[1] % U == 0:
                    bb, q = t[0], t[1] // U
                    g = NQ * bb + q
                    v.wait_ge(o_turned, g + 2)
                    o = ps[:, 7].rearrange("p (t h d) -> p t h d", t=NT, h=QH)
                    v.reciprocal(rden[:].rearrange("p (t h) -> p t h", t=NT), o[:, :, :, DH]).then_inc(rden_made, 1)
                    v.wait_ge(rden_made, g + 1)
                    dst = res[:, bass.ds(NT * bb, NT), q * QH * DH:(q + 1) * QH * DH]
                    v.tensor_tensor(dst.rearrange("p t (h d) -> p t h d", h=QH), o[:, :, :, 0:DH],
                                    rden[:].rearrange("p (t h) -> p t h", t=NT).unsqueeze(3)
                                    .broadcast_to([P, NT, QH, DH]), ALU.mult).then_inc(att_kept, 1)

            rounds(v, step)

            v.wait_ge(consts_in, 16 * 6)

            def residual(at):
                new, old = at(PROJ_LAG), at(NORM_LAG)
                if old:
                    v.wait_ge(stats_made, old[0] + 1)
                if new:
                    T, n, _ = new
                    v.wait_ge(out_projected, T + 1)
                    v.wait_ge(xb_made, T + 1)
                    v.tensor_tensor(hid[n % RING], ps[:, 2 + n % 2, 0:D], xb[n % RING], ALU.add).then_inc(sum_made, 1)
                if old:
                    st = stats[old[1] % RING]
                    v.bn_aggr(st[:, 6:8], st[:, 0:6]).then_inc(var_made, 1)
                if new:
                    v.wait_ge(sum_made, T + 1)
                    v.bn_stats(stats[n % RING][:, 0:6], hid[n % RING]).then_inc(stats_made, 1)
                if old:
                    T, n, b = old
                    r = n % RING
                    v.wait_ge(std_made, T + 1)
                    v.reciprocal(rstd[r][:], std[r][:]).then_inc(rstd_made, 1)
                    v.wait_ge(rstd_made, T + 1)
                    wait(v, x1_turned, T - RING + 1)
                    wait(v, x1_kept, T - RING + 1)
                    wait(v, x1_stored[r], 16 * (b * (CT // RING) + n // RING))
                    v.tensor_scalar(x1[r], hid[r], stats[r][:, 6:7], rstd[r][:], ALU.subtract, ALU.mult
                                    ).then_inc(x1_made, 1)

            tile_rounds(v, residual)

            steps = [0]

            def link(ins):
                steps[0] += 1
                ins.then_inc(route_step, 1)
                v.wait_ge(route_step, steps[0])

            def over_e(c):
                return c.unsqueeze(2).broadcast_to([P, TT, E])

            def over_t(c):
                return c.unsqueeze(1).broadcast_to([P, TT, E])

            r0, r1, r2, desc, r4, onehot = route
            v.wait_ge(logits_made, TT)
            link(v.tensor_tensor(r0, ps[:, 6, 0:TE].rearrange("p (t e) -> p t e", t=TT), over_t(br[:]), ALU.add))
            v.tensor_scalar(r1, r0, 50.0, -50.0, ALU.min, ALU.max).then_inc(logits_clipped, 1)
            v.wait_ge(probs_made, 1)
            v.wait_ge(iotas_made, 3)
            link(v.tensor_reduce(col[0], r2, AX_X, ALU.max))
            link(v.tensor_tensor(r0, r2, over_e(col[0]), ALU.is_equal))
            link(v.tensor_tensor(r4, r0, desc, ALU.mult))
            link(v.tensor_reduce(col[1], r4, AX_X, ALU.max))
            link(v.tensor_tensor(onehot, r4, over_e(col[1]), ALU.is_equal))
            v.tensor_copy(onehot_bf, onehot.rearrange("p t e -> p (t e)")).then_inc(onehot_made, 1)
            link(v.tensor_scalar(col[2], col[0], 1.0 - 1e-8, 1e-8, ALU.min, ALU.max))
            link(v.tensor_scalar(col[1], col[2], 0.5, 1e-8, ALU.add, ALU.add))
            link(v.tensor_scalar(col[3], col[1], 2.0, 0.5, ALU.min, ALU.max))
            link(v.reciprocal(col[0], col[3]))
            link(v.tensor_scalar(share[:], col[0], 0.5, None, ALU.mult))
            v.wait_ge(x1_kept, TT)
            link(v.tensor_tensor(res[:, 0:TT, D], col[2], col[0], ALU.mult))
            v.wait_ge(counted, 1)
            count, tiles, end, start = [stats[i][:, 0:E] for i in range(4)]
            link(v.tensor_reduce(count, ps[:, 1, 0:TE].rearrange("p (t e) -> p e t", t=TT), AX_X, ALU.add))
            link(v.tensor_tensor(need, count.unsqueeze(2).broadcast_to([P, E, TT]), step128, ALU.is_gt))
            link(v.tensor_reduce(end, need, AX_X, ALU.add))
            link(v.tensor_scalar(tiles, end, 1.0, None, ALU.max))
            link(v.tensor_copy(end, tiles))
            for e in range(1, E):
                link(v.tensor_tensor(end[:, e:e + 1], end[:, e - 1:e], tiles[:, e:e + 1], ALU.add))
            link(v.tensor_tensor(start, end, tiles, ALU.subtract))
            link(v.tensor_scalar(start, start, float(P), None, ALU.mult))
            link(v.tensor_scalar(ends[:], end[0:1], float(TT), None, ALU.add))
            link(v.tensor_tensor(r0, ps[:, 0, 0:TE].rearrange("p (t e) -> p t e", t=TT), over_t(start), ALU.add))
            link(v.tensor_tensor(r1, r0, onehot, ALU.mult))
            link(v.tensor_reduce(col[1], r1, AX_X, ALU.add))
            link(v.tensor_copy(pos[:], col[1]))
            link(v.tensor_tensor(tile_ge, tile_no, end[0:1].unsqueeze(1).broadcast_to([1, RT, E]), ALU.is_ge))
            link(v.tensor_reduce(tile_e[:], tile_ge[:, :, 0:E - 1], AX_X, ALU.add))
            link(v.tensor_scalar(tile_expert[:], tile_e[:], 1.0, None, ALU.add))
            v.tensor_scalar(tile_par[:], tile_expert[:], 1, None, ALU.bitwise_and).then_inc(routed, 1)

            def row(T):
                return res[:, bass.ds(T, 1), 0:D].rearrange("p o c -> p (o c)")

            def expert(s, par, shared):
                add = inside(s, SUM_LAG)
                sorted_ = add and not shared(SUM_LAG)
                t = s - SUM_LAG
                if add:
                    v.wait_ge(y_made, t + 1)
                if add and not sorted_:
                    if isinstance(s, int) and t == 0:
                        v.wait_ge(scattered, 16 * TT)
                    v.scalar_tensor_tensor(row(t), ps[:, 7, 0:D], share[:, bass.ds(t, 1)], row(t), ALU.mult, ALU.add
                                           ).then_inc(y_read, 1)
                if sorted_:
                    n = t - TT
                    rest_ = f_rest[1 - par]
                    if isinstance(s, int) and n == 0:
                        v.wait_ge(rest_scattered, 16 * TT)
                    v.wait_ge(f_rest_in[1 - par], 16 * (n // 2 + 1) if isinstance(n, int) else 8 * (n - (1 - par)) + 16)
                    v.scalar_tensor_tensor(f_sum[1 - par], ps[:, 7, 0:D], rest_[:, D:D + 1], rest_[:, 0:D], ALU.mult, ALU.add
                                           ).then_inc(y_read, 1)
                    v.tensor_copy(res[:, bass.ds(n, 1), D + 1:RW].rearrange("p o c -> p (o c)").bitcast(I32),
                                  rest_[:, D + 1:RW].bitcast(I32))
                if inside(s, 0):
                    v.wait_ge(fx_high, s + 1)
                    v.tensor_tensor(xl[par], ps[:, 0, 0:D].rearrange("p (k n) -> p k n", k=KD), xh[par].bitcast(F32),
                                    ALU.subtract).then_inc(fx_low, 1)
                if sorted_:
                    v.wait_ge(y_read, t + 1)
                    v.bn_stats(stats[1 - par][:, 0:6], f_sum[1 - par]).then_inc(sum_stats, 1)
                    v.wait_ge(sum_stats, n + 1)
                if inside(s, DOWN_LAG):
                    v.wait_ge(h_high, s - DOWN_LAG + 1)
                    v.tensor_tensor(hl, h_banks, hh.bitcast(F32), ALU.subtract).then_inc(h_low, 1)
                if sorted_:
                    v.bn_aggr(stats[1 - par][:, 6:8], stats[1 - par][:, 0:6]).then_inc(sum_stats2, 1)
                    v.wait_ge(sum_stats2, n + 1)
                    v.tensor_scalar(row(n), f_sum[1 - par], stats[1 - par][:, 6:7], None, ALU.subtract)
                    v.tensor_scalar(res[:, bass.ds(n, 1), D:D + 1].rearrange("p o c -> p (o c)"), stats[1 - par][:, 7:8],
                                    1.0, None, ALU.mult).then_inc(sum_kept, 1)
                if inside(s, UP_LAG):
                    u = s - UP_LAG
                    v.wait_ge(lin_up, u + 1)
                    v.wait_ge(silu_made, u + 1)
                    wait(v, h_turned, u - 1)
                    v.tensor_tensor(f_h[1 - par].rearrange("p (a n) -> p a n", a=2), f_s.rearrange("p (a n) -> p a n", a=2),
                                    ps[:, 3:5, 0:PIECE], ALU.mult).then_inc(h_made, 1)

            def check(a, b):
                c = CHECKS.index(b) + 1
                v.wait_ge(stds_made, c)
                v.reciprocal(rstd_all[:, a:b], std_all[:, a:b]).then_inc(rstds_made, 1)
                v.wait_ge(rstds_made, c)
                for t in range(a, b):
                    v.tensor_scalar(res[:, t, 0:D], res[:, t, 0:D], rstd_all[:, t:t + 1], None, ALU.mult).then_inc(normed, 1)

            ffn_steps(v, expert, check)

        @block.tensor
        def _(pe):
            pe.sem_inc(pv_done, NT)
            pe.sem_inc(o_turned, 1)
            pe.wait_ge(consts_made, 2)

            def project(i, par):
                b = 2 * i + par
                pe.wait_ge(x_loaded[par], 16 * (i + 1))
                wait(pe, xT_low, KD * b)
                for k in range(KD):
                    for n in range(NT):
                        mm = pe.transpose(ps[:, k, n * P:(n + 1) * P], x_in[par][:, n, k * P:(k + 1) * P], ident[:])
                mm.then_inc(x_turned, 1)
                if isinstance(b, int) and b == 0:
                    pe.wait_ge(wqkv_split, 2)
                pe.wait_ge(xT_low, KD * (b + 1))
                w_hi, w_lo = (w.rearrange("p (k n) -> p k n", k=KD) for w in (wqkv_hi, wqkv_lo))
                passes = ((xT_hi[par], w_hi), (xT_lo[par], w_hi), (xT_hi[par], w_lo))
                for m in range(4):
                    wait(pe, qk_read, 2 * (4 * b + m - 3))
                    for k in range(KD):
                        for i, (xp, wp) in enumerate(passes):
                            mm = pe.matmul(ps[:, 2 + m], wp[:, k, m * P:(m + 1) * P], xp[:, k],
                                           start=k == 0 and i == 0, stop=k == KD - 1 and i == 2)
                    mm.then_inc(qk_projected, 1)
                wait(pe, v_kept, 2 * b)
                for n in range(NT):
                    for k in range(KD):
                        for i, (xp, wp) in enumerate(passes):
                            mm = pe.matmul(ps[:, 6 + n // 2, (n % 2) * D:(n % 2 + 1) * D], xp[:, k, n * P:(n + 1) * P],
                                           wp[:, k, 2 * D:3 * D], start=k == 0 and i == 0, stop=k == KD - 1 and i == 2)
                mm.then_inc(v_projected, 1)

            project(0, 0)
            project(0, 1)
            with pe.Fori(1, B // 2) as i:
                project(i, 0)
                project(i, 1)

            pe.wait_ge(consts_made, 4)
            pe.wait_ge(v_kept, 2 * B)
            pe.wait_ge(qk_read, 8 * B)
            pe.wait_ge(ones_rows, NQ + 2)

            def step(b, s):
                if (t := item(b, s, 0)):
                    g, q, u = NQ * t[0] + t[1] // U, t[1] // U, t[1] % U
                    i, h0, n = M_UNITS[u]
                    w = (i + 1) * P
                    if u == 0:
                        pe.wait_ge(stack_loaded[q], 16 * 2 * NP_ * (t[0] + 1))
                    if not isinstance(g, int) or U * g + u >= SLOTS:
                        pe.wait_ge(max_found, U * g + u + 1 - SLOTS)
                    for a in range(n):
                        dst = ps[:, t[1] % SLOTS, a * w:(a + 1) * w]
                        pe.matmul(dst, q_st[q][0:SR, h0 + a, i * P:w], k_st[q][0:SR, h0 + a, 0:w], start=True, stop=False)
                        mm = pe.matmul(dst[:, i * P:w], ident_bf[:], mask_q[:], start=False, stop=True)
                    mm.then_inc(max_scored, 1)
                if (t := item(b, s, S_LAG)):
                    g, q, u = NQ * t[0] + t[1] // U, t[1] // U, t[1] % U
                    j, h0, n = S_UNITS[u]
                    w = S - j * P
                    if u == 0:
                        pe.wait_ge(m_placed, 16 * (g + 1))
                    pe.wait_ge(exped, U * g + u + 1)
                    for a in range(n):
                        mm = pe.matmul(ps[:, 3 + t[1] % SLOTS, a * w:(a + 1) * w], k_st[q][0:SM, h0 + a, j * P:(j + 1) * P],
                                       q_st[q][0:SM, h0 + a, j * P:S], start=True, stop=True)
                    mm.then_inc(scored, 1)
                if (t := item(b, s, PV_LAG)) and t[1] % U in S_LAST:
                    g, q, j = NQ * t[0] + t[1] // U, t[1] // U, S_LAST[t[1] % U]
                    pe.wait_ge(masked, NT * g + j + 1)
                    if j == 0:
                        pe.wait_ge(v_ready, g + 1)
                        pe.wait_ge(o_copied, g + 1)
                    for h in range(QH):
                        mm = pe.matmul(ps[32 * h:32 * h + 32, 6, j * P:S], v_ext[q % 2][:, j, h],
                                       probs[j][:, h], start=j == 0, stop=j == NT - 1)
                    mm.then_inc(pv_done, 1)
                if (t := item(b, s, M_TURN)) and t[1] % U == 0:
                    g = NQ * t[0] + t[1] // U
                    pe.wait_ge(m_split, g + 1)
                    wait(pe, att_kept, g - 1)
                    pe.transpose(ps[:, 7, 0:P // 2].bitcast(BF16), m_parts[:], ident_bf[:]).then_inc(m_turned, 1)
                if (t := item(b, s, O_TURN)) and t[1] % U == 0:
                    g = NQ * t[0] + t[1] // U
                    pe.wait_ge(o_copied, g + 2)
                    wait(pe, att_kept, g)
                    pe.wait_ge(m_copied, min(g + 2, QUADS) if isinstance(g, int) else g + 2)
                    for n in range(NT):
                        mm = pe.transpose(ps[:, 7, n * P:(n + 1) * P], o_sb[:, n * P:(n + 1) * P], ident[:])
                    mm.then_inc(o_turned, 1)

            rounds(pe, step)

            pe.wait_ge(att_kept, QUADS)

            def residual(at):
                if t := at(0):
                    T, n, _ = t
                    pe.wait_ge(att_staged, T + 1)
                    wait(pe, attT_copied, T - 1)
                    for k in range(KD):
                        mm = pe.transpose(ps[:, n % 2, k * P:(k + 1) * P], att_in[n % RING][:, k * P:(k + 1) * P], ident[:])
                    mm.then_inc(att_turned, 1)
                if t := at(PROJ_LAG):
                    T, n, _ = t
                    pe.wait_ge(attT_copied, T + 1)
                    wait(pe, sum_made, T - 1)
                    for k in range(KD):
                        mm = pe.matmul(ps[:, 2 + n % 2, 0:D], attT[n % RING][:, k], wo[:, k], start=k == 0, stop=k == KD - 1)
                    mm.then_inc(out_projected, 1)
                if t := at(X1_LAG):
                    T, n, _ = t
                    pe.wait_ge(x1_made, T + 1)
                    wait(pe, x1T_copied, T - 1)
                    for k in range(KD):
                        mm = pe.transpose(ps[:, 4 + n % 2, k * P:(k + 1) * P], x1[n % RING][:, k * P:(k + 1) * P], ident[:])
                    mm.then_inc(x1_turned, 1)
                if t := at(LOGIT_LAG):
                    T, n, _ = t
                    pe.wait_ge(x1T_copied, T + 1)
                    for k in range(KD):
                        mm = pe.matmul(ps[:, 6, bass.ds(T * E, E)], x1T[n % RING][:, k], wr[:, k], start=k == 0, stop=k == KD - 1)
                    mm.then_inc(logits_made, 1)

            tile_rounds(pe, residual)

            def rank_tokens():
                pe.wait_ge(onehot_made, 1)
                pe.matmul(ps[:, 0, 0:TE], before[:], onehot_bf, start=True, stop=False)
                for T in range(TT - 1):
                    left = TT - 1 - T
                    pe.matmul(ps[:, 0, (T + 1) * E:TE].rearrange("p (t e) -> p t e", t=left), ones_bf[:],
                              onehot_bf[:, T * E:(T + 1) * E].unsqueeze(1).broadcast_to([P, left, E]),
                              start=False, stop=T == TT - 2)
                pe.matmul(ps[:, 1, 0:TE], ones_bf[:], onehot_bf, start=True, stop=True).then_inc(counted, 1)

            rank_tokens()
            pe.wait_ge(routed, 1)

            pe.wait_ge(split_done, 1)

            def tile_set(t, lag, shared):
                if shared(lag):
                    return 0, 0
                at = bass.ds(t - TT, 1)
                return (pe.value_load(tile_expert[0:1, at], min_val=1, max_val=E),
                        pe.value_load(tile_par[0:1, at], min_val=0, max_val=1) * WBUF)

            def expert(s, par, shared):
                if inside(s, 0):
                    pe.wait_ge(fx_loaded[par], 8 * (s - par) + 16)
                    wait(pe, fx_low, s)
                    for k in range(KD):
                        mm = pe.transpose(ps[:, 0, k * P:(k + 1) * P], f_x[par][:, k * P:(k + 1) * P], ident[:])
                    mm.then_inc(fx_turned, 1)
                if inside(s, DOWN_LAG):
                    t = s - DOWN_LAG
                    pe.wait_ge(h_made, t + 1)
                    wait(pe, h_low, t)
                    for k in range(KI):
                        n = P if k < KI - 1 else LAST
                        mm = pe.transpose(ps[0:n, 5 + k // 4, k % 4 * P:(k % 4 + 1) * P], f_h[par][:, k * P:k * P + n], ident[:])
                    mm.then_inc(h_turned, 1)
                if inside(s, UP_LAG):
                    t = s - UP_LAG
                    w, at = tile_set(t, UP_LAG, shared)
                    if not shared(UP_LAG):
                        pe.wait_ge(split_done, w + 1)
                    pe.wait_ge(fx_low, t + 1)
                    x_hi, x_lo = xh[1 - par], xl[1 - par]
                    for half, bank, read, made in ((0, 1, silu_made, gate_up), (1, 3, h_made, lin_up)):
                        wait(pe, read, t)
                        for k in range(KD):
                            for i, (xp, low) in enumerate(((x_hi, 0), (x_hi, SLOT), (x_lo, 0))):
                                for a in range(2):
                                    mm = pe.matmul(ps[:, bank + a, 0:PIECE], xp[:, k],
                                                   w_split[:, bass.ds(at + low + k * UP + half * I + a * PIECE, PIECE)],
                                                   start=k == 0 and i == 0, stop=k == KD - 1 and i == 2)
                        mm.then_inc(made, 1)
                if inside(s, DOWN_LAG):
                    t = s - DOWN_LAG
                    _, at = tile_set(t, DOWN_LAG, shared)
                    pe.wait_ge(h_low, t + 1)
                    wait(pe, y_read, t)
                    for k in range(KI):
                        n = P if k < KI - 1 else LAST
                        for i, (hp, low) in enumerate(((hh, 0), (hh, SLOT), (hl, 0))):
                            mm = pe.matmul(ps[:, 7, 0:D], hp[0:n, k], w_split[0:n, bass.ds(at + low + UPW + k * D, D)],
                                           start=k == 0 and i == 0, stop=k == KI - 1 and i == 2)
                    mm.then_inc(y_made, 1)

            ffn_steps(pe, expert)


def kernel(**inputs):
    import numpy as np
    import concourse.bacc as bacc
    from concourse import mybir as mb
    from concourse.bass_utils import run_bass_kernel_spmd

    a = {k.replace("L0_", ""): np.asarray(t) for k, t in inputs.items()}

    def by_rows(w):
        return w.reshape(*w.shape[:-2], -1, P, w.shape[-1]).swapaxes(-3, -2)

    def on_all(t):
        return np.broadcast_to(t, (P, t.size))

    sets = {}
    for n in (1, 2, 3):
        w = np.concatenate([a[f"ffn_sw{n}"][None], a[f"ffn_ew{n}"]])
        sets[n] = w.transpose(0, 2, 1)
    up = by_rows(np.concatenate([sets[1], sets[3]], axis=2)).reshape(NW, P, UPW)
    down = np.zeros((NW, KI * P, D), np.float32)
    down[:, :I] = sets[2]
    down = by_rows(down).reshape(NW, P, DNW)
    laid = {
        "x": a["attn_x"].reshape(TT, P, D),
        "w_qkv": by_rows(np.concatenate([a["attn_w_q"], a["attn_w_k"], a["attn_w_v"]], axis=1)),
        "b_qk": np.concatenate([a["attn_b_q"], a["attn_b_k"]]).reshape(4, P).T,
        "b_v": on_all(a["attn_b_v"]),
        "w_o": by_rows(a["attn_w_o"]),
        "b_o": on_all(a["attn_b_o"]),
        "w_r": by_rows(a["ffn_router_w"].T),
        "b_r": on_all(a["ffn_routing_bias"]),
        "w_sets": np.concatenate([up, down], axis=2),
    }
    nc = bacc.Bacc("TRN2", target_bir_lowering=False, num_devices=1)
    arrays, args = {}, {}
    for name, t in laid.items():
        arrays[f"in_{name}"] = np.ascontiguousarray(t)
        args[name] = nc.dram_tensor(f"in_{name}", t.shape, mb.dt.float32, kind="ExternalInput").ap()
    out = nc.dram_tensor("out_rows", (TOK, D), mb.dt.float32, kind="ExternalOutput").ap()
    block_kernel(nc, **args, out=out)
    r = run_bass_kernel_spmd(nc, [arrays], core_ids=[0])
    return r.results[0]["out_rows"].reshape(B, S, D)
```

```python
from contextlib import ExitStack

import concourse.bass as bass
from concourse import mybir

ALU = mybir.AluOpType
ACT = mybir.ActivationFunctionType
AX_X = mybir.AxisListType.X
F32 = mybir.dt.float32
F32R = mybir.dt.float32r
BF16 = mybir.dt.bfloat16
I32 = mybir.dt.int32
U32 = mybir.dt.uint32

P = 128
B, S, D = 8, 512, 256
H, DH = 16, 16
TOK = B * S
TT = TOK // P
NT = S // P
KD = D // P
QH = 4
NQ = H // QH
QUADS = B * NQ
I, E = 704, 7
NW = E + 1
UP = 2 * I
KI = -(-I // P)
LAST = I - (KI - 1) * P
UPW, DNW = KD * UP, KI * D
SLOT = UPW + DNW
PIECE = I // 2
RT = TT + E
SORTED = RT * P
RW = D + 2
SCALE = 0.25
EPS = 1e-5
MASKED = -1e30
K_PARTS = (0, 0, 1, 1, 0, 2)
Q_PARTS = (0, 1, 0, 1, 2, 0)
NP_ = len(K_PARTS)
SR = NP_ * DH
SM = SR + 3


def wait(eng, sem, count):
    if not isinstance(count, int) or count > 0:
        eng.wait_ge(sem, count)


def block_kernel(nc, x, w_qkv, b_qk, b_v, w_o, b_o, w_r, b_r, w_sets, out):
    with ExitStack() as ctx:
        def sb(name, shape, dt=F32):
            return ctx.enter_context(nc.sbuf_tensor(name, shape, dt))

        def sem(name):
            return ctx.enter_context(nc.semaphore(name))

        qk_parts = nc.dram_tensor("qk_parts", [2, 3, QUADS * QH * DH, S], BF16, kind="Internal").ap()
        rows_in = nc.dram_tensor("rows_in", [SORTED, D], F32, kind="Internal").ap()
        rows_rest = nc.dram_tensor("rows_rest", [SORTED, RW], F32, kind="Internal").ap()

        arena_at = -(-nc.sbuf_base // 32) * 32
        arena = sb("arena", [P, 8 * SLOT + 5632])
        WBUF = 4 * SLOT
        RAW, SCRATCH, WORK = 2 * SLOT, 4 * SLOT, 8 * SLOT
        AR = 4

        def placed(name, words, at, dt=F32R):
            return nc.alloc_sbuf_tensor_at(name, [P, words], dt, offset=arena_at + 4 * at)

        w_split = placed("w_split", WBUF + 2 * SLOT, 0)
        raw = [placed(f"raw{i}", SLOT, RAW + i * SLOT, F32)[:] for i in range(2)]
        raw_shared = placed("raw_shared", SLOT, SLOT, F32)[:]

        place = [0]

        def carve(words):
            at = place[0]
            place[0] += words
            assert at >= WORK or place[0] <= WORK
            assert place[0] <= WORK + 5632
            return arena[:, at:at + words]

        def carve_r(name, words):
            carve(words)
            return placed(name, words, place[0] - words)

        place[0] = RAW
        xb = carve(TT * D).rearrange("p (t c) -> p t c", t=TT)
        place[0] = 0
        x_in = [carve(NT * D).rearrange("p (n c) -> p n c", n=NT) for _ in range(2)]
        xT_hi = [carve_r(f"xT_hi{i}", KD * S)[:].rearrange("p (k n) -> p k n", k=KD) for i in range(2)]
        xT_lo = [carve_r(f"xT_lo{i}", KD * S)[:].rearrange("p (k n) -> p k n", k=KD) for i in range(2)]
        qk32 = [carve(S) for _ in range(AR)]
        assert place[0] <= RAW
        place[0] = SCRATCH
        v_all = carve(B * NT * D).rearrange("p (b n c) -> p b n c", b=B, n=NT)
        stack = lambda: carve(QH * S // 2).bitcast(BF16).rearrange("p (h n) -> p h n", h=QH)
        early = [(stack(), stack()) for _ in range(2)]
        shared_at = place[0]
        rest = [carve(S) for _ in range(AR)]
        parts = [carve(3 * S // 2).bitcast(BF16).rearrange("p (t n) -> p t n", t=3) for _ in range(AR)]
        assert place[0] <= WORK
        place[0] = WORK
        wqkv = carve(KD * 3 * D)
        wqkv_hi = carve_r("wqkv_hi", KD * 3 * D)[:]
        wqkv_lo = carve_r("wqkv_lo", KD * 3 * D)[:]
        wo = carve(KD * D)
        bv = carve(D)
        place[0] = shared_at
        q_st, k_st = zip(*early, *((stack(), stack()) for _ in range(2, NQ)))
        v_ext = [carve(QH * S // 4).rearrange("p (n h d) -> p n h d", n=NT, h=QH) for _ in range(2)]
        place[0] = WORK
        probs = [carve(QH * (S - j * P)).rearrange("p (h n) -> p h n", h=QH) for j in range(NT)]
        o_sb = carve(S)
        RING = 5
        place[0] = SCRATCH
        attT_hi, attT_lo = ([carve_r(f"attT_{part}{i}", D)[:].rearrange("p (k n) -> p k n", k=KD) for i in range(RING)]
                            for part in ("hi", "lo"))
        hid = [carve(D) for _ in range(RING)]
        x1T = [carve(D).rearrange("p (k n) -> p k n", k=KD) for _ in range(RING)]
        xh = [placed(f"xh{i}", D, 6 * SLOT + i * D)[:].rearrange("p (k n) -> p k n", k=KD) for i in range(2)]
        xl = [placed(f"xl{i}", D, 6 * SLOT + (2 + i) * D)[:].rearrange("p (k n) -> p k n", k=KD) for i in range(2)]
        hh = placed("hh", KI * P, 6 * SLOT + 4 * D)[:].rearrange("p (k n) -> p k n", k=KI)
        hl = placed("hl", KI * P, 6 * SLOT + 4 * D + KI * P)[:].rearrange("p (k n) -> p k n", k=KI)
        place[0] = 6 * SLOT + 4 * D + 2 * KI * P
        f_x_at = place[0]
        f_x = [carve(D) for _ in range(2)]
        f_s = carve(I)
        f_h = [carve(KI * P) for _ in range(2)]
        f_rest = [carve(RW) for _ in range(2)]
        f_sum = [carve(D) for _ in range(2)]

        res = sb("res", [P, RT, RW])

        ident = sb("ident", [P, P])
        ident_bf = sb("ident_bf", [P, P], BF16)
        zeros = sb("zeros", [P, D])
        mask_q = sb("mask_q", [P, P], BF16)
        before = sb("before", [P, P], BF16)
        ones_bf = sb("ones_bf", [P, P], BF16)
        bqk = sb("bqk", [P, 4])
        template = sb("template", [P, RW])
        bo = sb("bo", [P, D])
        wo_hi = sb("wo_hi", [P, KD, D], F32R)
        wo_lo = sb("wo_lo", [P, KD, D], F32R)
        wr = sb("wr", [P, KD, E])
        br = sb("br", [P, E])
        negmax = [sb(f"negmax{i}", [P, QH * NT]) for i in range(2)]
        idle = sb("idle", [P, 1])
        m_rest = sb("m_rest", [P, QH * NT])
        m_parts = sb("m_parts", [P, P], BF16)
        m_rows = sb("m_rows", [3 * QH * NT, P], BF16)
        rden = sb("rden", [P, NT * QH])
        stats = [sb(f"stats{i}", [P, 8]) for i in range(RING)]
        std = [sb(f"std{i}", [P, 1]) for i in range(RING)]
        eps = sb("eps", [P, 1])
        rstd = [sb(f"rstd{i}", [P, 1]) for i in range(RING)]
        TE = TT * E
        place[0] = SCRATCH + 4 * RING * D
        grid = lambda t: t.rearrange("p (t e) -> p t e", t=TT)
        route = [grid(carve(TT * E)) for _ in range(6)]
        onehot_bf = carve(TT * E // 2).bitcast(BF16)
        col = [carve(TT) for _ in range(4)]
        share = sb("share", [P, TT])
        pos = sb("pos", [P, TT], U32)
        std_all = sb("std_all", [P, RT])
        ends = sb("ends", [1, E], I32)
        need = carve(E * TT).rearrange("p (e t) -> p e t", e=E)
        step128 = carve(E * TT).rearrange("p (e t) -> p e t", e=E)
        tile_no = carve(RT * E)[0:1].rearrange("p (t e) -> p t e", t=RT)
        tile_ge = carve(RT * E)[0:1].rearrange("p (t e) -> p t e", t=RT)
        tile_e = carve(RT)[0:1]
        tile_expert = sb("tile_expert", [1, RT], I32)
        assert place[0] <= f_x_at - 2 * KI * P - 4 * D

        ps = ctx.enter_context(nc.psum_tensor("ps", [P, 8, 512], F32))

        consts_in = sem("consts_in")
        wqkv_in = sem("wqkv_in")
        consts_made = sem("consts_made")
        pool_step = sem("pool_step")
        x_loaded = [sem(f"x_loaded{i}") for i in range(2)]
        x_turned = sem("x_turned")
        wqkv_split = sem("wqkv_split")
        xT_copied = sem("xT_copied")
        xT_low = sem("xT_low")
        qk_projected = sem("qk_projected")
        v_projected = sem("v_projected")
        qk_read = sem("qk_read")
        rest_made = sem("rest_made")
        mid_made = sem("mid_made")
        low_made = sem("low_made")
        v_kept = sem("v_kept")
        parts_stored = [sem(f"parts_stored{i}") for i in range(AR)]
        x_again = [sem(f"x_again{i}") for i in range(2)]
        xb_made = sem("xb_made")
        stack_loaded = [sem(f"stack_loaded{i}") for i in range(NQ)]
        ones_rows = sem("ones_rows")
        v_ones = sem("v_ones")
        max_scored = sem("max_scored")
        max_found = sem("max_found")
        m_step = sem("m_step")
        m_split = sem("m_split")
        m_turned = sem("m_turned")
        m_copied = sem("m_copied")
        m_placed = sem("m_placed")
        scored = sem("scored")
        exped = sem("exped")
        masked = sem("masked")
        v_ready = sem("v_ready")
        pv_done = sem("pv_done")
        o_copied = sem("o_copied")
        o_turned = sem("o_turned")
        rden_made = sem("rden_made")
        att_kept = sem("att_kept")
        raw_in = [sem(f"raw_in{i}") for i in range(2)]
        split_step = sem("split_step")
        split_done = sem("split_done")
        template_made = sem("template_made")
        zero_rows = sem("zero_rows")
        att_turned = sem("att_turned")
        wo_split = sem("wo_split")
        attT_copied = sem("attT_copied")
        attT_low = sem("attT_low")
        out_projected = sem("out_projected")
        sum_made = sem("sum_made")
        stats_made = sem("stats_made")
        var_made = sem("var_made")
        rstd_made = sem("rstd_made")
        std_made = sem("std_made")
        x1_made = sem("x1_made")
        x1_turned = sem("x1_turned")
        x1T_copied = sem("x1T_copied")
        logits_made = sem("logits_made")
        iotas_made = sem("iotas_made")
        logits_clipped = sem("logits_clipped")
        probs_made = sem("probs_made")
        onehot_made = sem("onehot_made")
        counted = sem("counted")
        route_step = sem("route_step")
        routed = sem("routed")
        scattered = [sem(f"scattered{i}") for i in range(2)]
        fx_loaded = [sem(f"fx_loaded{i}") for i in range(2)]
        fx_turned = sem("fx_turned")
        fx_high = sem("fx_high")
        fx_low = sem("fx_low")
        gate_up = sem("gate_up")
        lin_up = sem("lin_up")
        silu_made = sem("silu_made")
        h_made = sem("h_made")
        h_turned = sem("h_turned")
        h_high = sem("h_high")
        h_low = sem("h_low")
        y_made = sem("y_made")
        y_read = sem("y_read")
        rest_scattered = sem("rest_scattered")
        f_rest_in = [sem(f"f_rest_in{i}") for i in range(2)]
        sum_stats = sem("sum_stats")
        sum_stats2 = sem("sum_var")
        sum_kept = sem("sum_kept")
        stds_made = sem("stds_made")
        rstds_made = sem("rstds_made")
        normed = sem("normed")
        out_scattered = sem("out_scattered")

        h_banks = ps[:, 5:7].rearrange("p a n -> p (a n)")[:, 0:KI * P].rearrange("p (k n) -> p k n", k=KI)
        qk_rows = QH * DH
        qk_store = qk_parts.rearrange("w t r n -> w r t n")

        block = ctx.enter_context(nc.Block())

        M_UNITS = [(i, h, n) for i in range(NT) for n in (2 if i < NT // 2 else 1,) for h in range(0, QH, n)]
        S_UNITS = [(j, h, n) for j in range(NT) for n in (1 if j < NT // 2 else 2,) for h in range(0, QH, n)]
        U = len(M_UNITS)
        SLOTS = 3
        STEPS = NQ * U
        assert STEPS % SLOTS == 0
        S_LAST = {max(u for u in range(U) if S_UNITS[u][0] == j): j for j in range(NT)}
        M_TURN, S_LAG, V_LAG = 17, 22, 16
        PV_LAG, O_COPY, O_TURN = S_LAG + 4, S_LAG + 15, S_LAG + 17

        def item(b, s, lag):
            d, n = divmod(s - lag, STEPS)
            if isinstance(b, int) and not 0 <= b + d < B:
                return None
            if lag == 0 and d < 0:
                return None
            return b + d, n

        LOW_LAG, PROJ_LAG, STD_LAG, NORM_LAG, X1_LAG, LOGIT_LAG = 1, 2, 3, 4, 5, 6

        def tile_rounds(body):
            for s in range(TT + LOGIT_LAG):
                body(lambda lag: s - lag if 0 <= s - lag < TT else None)

        FT = TT + RT
        UP_LAG, DOWN_LAG, SUM_LAG = 1, 2, 3
        STEADY = 4
        CHECKS = (14, 24, 34, 36, RT)

        def ffn_steps(eng, body, check=None):
            def one(s, par, first):
                body(s, par, lambda lag: first - lag < TT)

            def straight(a, b):
                for s in range(a, b):
                    one(s, s % 2, s)

            def loop(a, b):
                if a == b:
                    return
                kind = STEADY if b <= TT else TT + STEADY
                with eng.Fori(a // 2, b // 2) as i:
                    for par in range(2):
                        one(2 * i + par, par, kind + par)

            straight(0, STEADY)
            loop(STEADY, TT)
            straight(TT, TT + STEADY)
            at, done = TT + STEADY, 0
            for c in CHECKS[:-2]:
                end = TT + c + SUM_LAG + 1
                loop(at, end)
                if check:
                    check(done, c)
                at, done = end, c
            last = FT // 2 * 2
            loop(at, last)
            straight(last, last + 1)
            if check:
                check(done, CHECKS[-2])
            done = CHECKS[-2]
            straight(last + 1, FT + SUM_LAG + 1)
            if check:
                check(done, RT)

        def batches(eng, turn, project):
            turn(0, 0)
            turn(0, 1)
            project(0, 0)
            with eng.Fori(1, B // 2) as i:
                turn(i, 0)
                project(i - 1, 1)
                turn(i, 1)
                project(i, 0)
            project(B // 2 - 1, 1)

        def inside(s, lag):
            return not isinstance(s, int) or 0 <= s - lag < FT

        def rounds(eng, body):
            def one(b):
                for s in range(STEPS):
                    body(b, s)
            one(0)
            with eng.Fori(1, B) as b:
                one(b)
            one(B)

        @block.sync
        def _(sp):
            sp.dma_start(wqkv, w_qkv.rearrange("p k n -> p (k n)")).then_inc(wqkv_in, 16)

            def proj_batch(i, par):
                b = 2 * i + par
                wait(sp, x_turned, b - 1)
                tiles = x[bass.ds(b * NT, NT)].rearrange("n p c -> p n c")
                sp.dma_start(x_in[par], tiles).then_inc(x_loaded[par], 16)
                sp.dma_start(xb[:, bass.ds(b * NT, NT)], tiles).then_inc(x_again[par], 16)

            def store_batch(b):
                for m in range(4):
                    sp.wait_ge(low_made, 4 * b + m + 1)
                    sp.dma_start(qk_store[m // 2, bass.ds((4 * b + 2 * (m % 2)) * qk_rows, P)],
                                 parts[m]).then_inc(parts_stored[m], 16)

            proj_batch(0, 0)
            for dst, src in ((bqk[:], b_qk), (bv, b_v), (bo[:], b_o), (br[:], b_r),
                             (wo, w_o.rearrange("p k n -> p (k n)")), (wr[:], w_r)):
                sp.dma_start(dst, src).then_inc(consts_in, 16)
            proj_batch(0, 1)
            with sp.Fori(1, B // 2) as i:
                proj_batch(i, 0)
                store_batch(2 * i - 2)
                proj_batch(i, 1)
                store_batch(2 * i - 1)

            def load_stack(b, q):
                wait(sp, scored, U * (NQ * b + q - NQ + 1))
                for t in range(NP_):
                    for side, st, which in ((0, q_st, Q_PARTS), (1, k_st, K_PARTS)):
                        src = qk_parts[side, which[t], bass.ds((NQ * b + q) * qk_rows, qk_rows)]
                        sp.dma_start(st[q][t * DH:(t + 1) * DH], src.rearrange("(h d) n -> d h n", h=QH)
                                     ).then_inc(stack_loaded[q], 16)

            def place_max(b, q):
                sp.wait_ge(m_copied, NQ * b + q + 1)
                sp.dma_start(q_st[q][SR:SM].rearrange("p h n -> p (h n)"), m_rows[:]).then_inc(m_placed, 16)

            for i in range(AR):
                sp.wait_ge(parts_stored[i], 16 * (B - 3))
            load_stack(0, 0)
            store_batch(B - 2)
            load_stack(0, 1)
            store_batch(B - 1)

            for i in range(AR):
                sp.wait_ge(parts_stored[i], 16 * B)
            sp.wait_ge(template_made, 2)

            def fill(b):
                n = -(-RT // B)
                for dst, w in ((rows_in, D), (rows_rest, RW)):
                    first = b * n if isinstance(b, int) and b * n + n <= RT else b * n if not isinstance(b, int) else RT - n
                    rows = dst[bass.ds(first * P, n * P)].rearrange("(t p) c -> p t c", p=P)
                    sp.dma_start(rows, template[:, 0:w].unsqueeze(1).broadcast_to([P, n, w])).then_inc(zero_rows, 16)

            def stacks(b):
                for q in range(NQ):
                    if q < 2:
                        load_stack(b, q + 2)
                    elif not (isinstance(b, int) and b == B - 1):
                        load_stack(b + 1, q - 2)
                    place_max(b, q)
                fill(b)

            stacks(0)
            with sp.Fori(1, B - 1) as b:
                stacks(b)
            stacks(B - 1)
            def expert(s, par, shared):
                if inside(s, 0):
                    if isinstance(s, int) and s <= 2:
                        sp.wait_ge(x1_made, (1, 2, TT)[s])
                    if isinstance(s, int) and s == TT:
                        for i in range(2):
                            sp.wait_ge(scattered[i], 16 * (TT // 2))
                    wait(sp, fx_turned, s - 1)
                    src = (res[:, bass.ds(s, 1), 0:D].rearrange("p o c -> p (o c)") if shared(0) else
                           rows_in[bass.ds((s - TT) * P, P)])
                    sp.dma_start(f_x[par], src).then_inc(fx_loaded[par], 16)
                if inside(s, DOWN_LAG) and not shared(DOWN_LAG):
                    t = s - DOWN_LAG
                    if isinstance(t, int) and t == TT:
                        sp.wait_ge(rest_scattered, 16 * TT)
                    wait(sp, sum_kept, t - TT - 1)
                    sp.dma_start(f_rest[par], rows_rest[bass.ds((t - TT) * P, P)]).then_inc(f_rest_in[par], 16)

            ffn_steps(sp, expert)
            sp.wait_ge(out_scattered, 16 * RT)

        @block.gpsimd
        def _(pool):
            pool.memset(zeros[:], 0.0).then_inc(pool_step, 1)
            pool.memset(ones_bf[:], 1.0).then_inc(pool_step, 1)
            pool.memset(m_parts[:], 0.0).then_inc(pool_step, 1)
            pool.memset(eps[:], EPS).then_inc(pool_step, 1)
            pool.memset(template[:], 0.0).then_inc(pool_step, 1)
            pool.wait_ge(pool_step, 5)
            z = zeros[:, 0:P]
            for dst in (ident, ident_bf):
                pool.affine_select(dst[:], z, [[-1, P]], ALU.not_equal, 1.0, 0, 1).then_inc(consts_made, 1)
            pool.wait_ge(wqkv_in, 16)
            pool.tensor_copy(wqkv_hi, wqkv).then_inc(wqkv_split, 1)
            pool.wait_ge(wqkv_split, 1)
            pool.tensor_tensor(wqkv_lo, wqkv, wqkv_hi.bitcast(F32), ALU.subtract).then_inc(wqkv_split, 1)
            pool.affine_select(mask_q[:], z, [[-1, P]], ALU.is_ge, MASKED, 0, 1).then_inc(consts_made, 1)
            pool.affine_select(before[:], ones_bf[:], [[1, P]], ALU.is_gt, 0.0, 0, -1).then_inc(consts_made, 1)
            pool.iota(template[:, D + 1:RW].bitcast(I32), [[0, 1]], 1 << 20, 0).then_inc(template_made, 1)
            pool.iota(res[:, 0:TT, D + 1:RW].bitcast(I32), [[P, TT], [0, 1]], 0, 1).then_inc(template_made, 1)

            def load_set(w):
                pool.dma_start(raw[w % 2] if w else raw_shared, w_sets[w]).then_inc(raw_in[w % 2], 16)

            def split_set(w):
                at = w % 2 * WBUF
                src = raw[w % 2] if w else raw_shared
                pool.wait_ge(raw_in[w % 2], 16 * (w // 2 + 1))
                pool.tensor_tensor(w_split[:, at:at + SLOT], src, zeros[:, 0:1].broadcast_to([P, SLOT]), ALU.add
                                   ).then_inc(split_step, 1)
                pool.wait_ge(split_step, w + 1)
                pool.tensor_tensor(w_split[:, at + SLOT:at + 2 * SLOT], src, w_split[:, at:at + SLOT].bitcast(F32),
                                   ALU.subtract).then_inc(split_done, 1)
                if 0 < w < NW - 2:
                    pool.wait_ge(split_done, w + 1)
                    load_set(w + 2)

            def middle(b):
                for m in range(4):
                    pool.wait_ge(rest_made, 4 * b + m + 1)
                    pool.tensor_tensor(parts[m][:, 1], rest[m], zeros[:, 0:1].broadcast_to([P, S]),
                                       ALU.add).then_inc(mid_made, 1)

            pool.wait_ge(consts_in, 16 * 6)
            pool.tensor_tensor(wo_hi[:].rearrange("p k n -> p (k n)"), wo, zeros[:, 0:1].broadcast_to([P, KD * D]), ALU.add
                               ).then_inc(wo_split, 1)
            pool.wait_ge(wo_split, 1)
            pool.tensor_tensor(wo_lo[:].rearrange("p k n -> p (k n)"), wo, wo_hi[:].bitcast(F32).rearrange("p k n -> p (k n)"),
                               ALU.subtract).then_inc(wo_split, 1)
            with pool.Fori(0, B) as b:
                middle(b)

            def attend(b, s):
                if isinstance(b, int) and b == 0 and s == U:
                    for i in range(AR):
                        pool.wait_ge(parts_stored[i], 16 * B)
                    for i in range(2):
                        pool.memset(v_ext[i][:, :, :, DH:2 * DH], 1.0).then_inc(v_ones, 1)
                    pool.wait_ge(v_ones, 2)
                    for q in range(2, NQ):
                        pool.memset(k_st[q][SR:SM], 1.0).then_inc(ones_rows, 1)
                    pool.wait_ge(ones_rows, NQ)
                if isinstance(b, int) and b == 0 and s == STEPS // 2:
                    pool.wait_ge(v_projected, B)
                    pool.wait_ge(rest_made, 4 * B)
                    load_set(0)
                if (t := item(b, s, V_LAG)) and t[1] % U == 0:
                    g, q = NQ * t[0] + t[1] // U, t[1] // U
                    wait(pool, pv_done, NT * g if not isinstance(g, int) or g > 1 else 0)
                    pool.wait_ge(v_kept, 2 * B)
                    pool.tensor_copy(v_ext[q % 2][:, :, :, 0:DH],
                                     v_all[:, bass.ds(t[0], 1), :, q * QH * DH:(q + 1) * QH * DH]
                                     .rearrange("p o n (h d) -> p (o n) h d", h=QH)).then_inc(v_ready, 1)
                if (t := item(b, s, S_LAG)) and t[1] % U in S_LAST:
                    g, j = NQ * t[0] + t[1] // U, S_LAST[t[1] % U]
                    wait(pool, masked, NT * g + j)
                    pool.wait_ge(exped, U * g + t[1] % U + 1 + SLOTS)
                    pool.tensor_tensor(idle[:], zeros[:, 0:1], zeros[:, 0:1], ALU.add)
                    diagonal = probs[j][:, :, 0:P]
                    pool.affine_select(diagonal, diagonal, [[0, QH], [1, P]], ALU.is_ge, 0.0, 0, -1).then_inc(masked, 1)
                if (t := item(b, s, U - 1)) and t[1] % U == 0:
                    g, q = NQ * t[0] + t[1] // U, t[1] // U
                    pool.wait_ge(max_found, U * (g + 1))
                    wait(pool, m_turned, g)
                    n = QH * NT
                    nm = negmax[q % 2]
                    none = zeros[:, 0:n]
                    pool.tensor_tensor(m_parts[:, 0:n], nm[:], none, ALU.add).then_inc(m_step, 1)
                    pool.wait_ge(m_step, 3 * g + 1)
                    pool.tensor_tensor(m_rest[:], nm[:], m_parts[:, 0:n], ALU.subtract).then_inc(m_step, 1)
                    pool.wait_ge(m_step, 3 * g + 2)
                    pool.tensor_tensor(m_parts[:, n:2 * n], m_rest[:], none, ALU.add).then_inc(m_step, 1)
                    pool.wait_ge(m_step, 3 * g + 3)
                    pool.tensor_tensor(m_parts[:, 2 * n:3 * n], m_rest[:], m_parts[:, n:2 * n],
                                       ALU.subtract).then_inc(m_split, 1)

            rounds(pool, attend)

            pool.wait_ge(consts_in, 16 * 6)
            for i in range(2):
                pool.wait_ge(x_again[i], 16 * (B // 2))
            for b in range(B):
                some = xb[:, b * NT:(b + 1) * NT]
                pool.tensor_tensor(some, some, bo[:].unsqueeze(1).broadcast_to([P, NT, D]), ALU.add).then_inc(xb_made, 1)
            split_set(0)

            pool.iota(route[3], [[0, TT], [-1, E]], E + 1, 0, allow_small_or_imprecise_dtypes=True).then_inc(iotas_made, 1)
            pool.iota(step128, [[0, E], [P, TT]], 0, 0, allow_small_or_imprecise_dtypes=True).then_inc(iotas_made, 1)
            pool.iota(tile_no, [[1, RT], [0, E]], 0, 0, allow_small_or_imprecise_dtypes=True).then_inc(iotas_made, 1)
            pool.wait_ge(routed, 1)
            pool.wait_ge(x1_made, TT)
            pool.wait_ge(zero_rows, 32 * B)
            for T in range(TT):
                if T >= 2:
                    pool.wait_ge(scattered[T % 2], 16 * (T // 2))
                pool.indirect_dma_start(rows_in, bass.IndirectOffsetOnAxis(ap=pos[:, T:T + 1], axis=0),
                                        res[:, T, 0:D], None).then_inc(scattered[T % 2], 16)
            load_set(1)
            load_set(2)
            split_set(1)
            for T in range(TT):
                pool.wait_ge(y_read, T + 1)
                pool.indirect_dma_start(rows_rest, bass.IndirectOffsetOnAxis(ap=pos[:, T:T + 1], axis=0),
                                        res[:, T], None).then_inc(rest_scattered, 16)
            split_set(2)
            for w in range(3, NW):
                done = pool.value_load(ends[0:1, w - 3:w - 2], min_val=TT + 1, max_val=FT)
                pool.wait_ge(y_made, done)
                pool.tensor_tensor(idle[:], zeros[:, 0:1], zeros[:, 0:1], ALU.add)
                split_set(w)
            for t in range(RT):
                pool.wait_ge(normed, t + 1)
                pool.indirect_dma_start(out, bass.IndirectOffsetOnAxis(ap=res[:, t, D + 1:RW].bitcast(U32), axis=0),
                                        res[:, t, 0:D], None, bounds_check=TOK - 1, oob_is_err=False
                                        ).then_inc(out_scattered, 16)

        @block.scalar
        def _(act):
            act.sem_inc(exped, SLOTS)
            act.sem_inc(o_copied, 1)
            act.wait_ge(consts_in, 16 * 6)

            def high_parts(i, par):
                b = 2 * i + par
                act.wait_ge(x_turned, b + 1)
                wait(act, v_projected, b - 1)
                for k in range(KD):
                    act.activation(xT_hi[par][:, k], ps[:, k], ACT.Copy).then_inc(xT_copied, 1)

            def project(i, par):
                b = 2 * i + par
                for m in range(4):
                    n = 4 * b + m
                    act.wait_ge(qk_projected, n + 1)
                    wait(act, rest_made, n - AR + 1)
                    act.activation(qk32[m], ps[:, 2 + m], ACT.Identity, bias=bqk[:, m:m + 1]).then_inc(qk_read, 1)
                    wait(act, parts_stored[m], 16 * b)
                    act.activation(parts[m][:, 0], ps[:, 2 + m], ACT.Identity, bias=bqk[:, m:m + 1]).then_inc(qk_read, 1)

            batches(act, high_parts, project)

            act.wait_ge(wo_split, 2)

            def step(b, s):
                if (t := item(b, s, O_COPY)) and t[1] % U == 0:
                    g = NQ * t[0] + t[1] // U
                    act.wait_ge(pv_done, NT * (g + 2))
                    act.wait_ge(o_turned, g + 1)
                    act.activation(o_sb, ps[:, 6], ACT.Copy).then_inc(o_copied, 1)
                if (t := item(b, s, S_LAG)):
                    g, u = NQ * t[0] + t[1] // U, t[1] % U
                    j, h, n = S_UNITS[u]
                    w = S - j * P
                    act.wait_ge(scored, U * g + u + 1)
                    act.wait_ge(pv_done, NT * g + j + 1)
                    act.activation(probs[j][:, h:h + n], ps[:, 3 + t[1] % SLOTS, 0:n * w].rearrange("p (h n) -> p h n", h=n),
                                   ACT.Exp, scale=SCALE).then_inc(exped, 1)
                if (t := item(b, s, M_TURN)) and t[1] % U == 0:
                    g = NQ * t[0] + t[1] // U
                    act.wait_ge(m_turned, g + 1)
                    wait(act, m_placed, 16 * g)
                    n = 3 * QH * NT
                    act.activation(m_rows[:], ps[0:n, 7, 0:P // 2].bitcast(BF16), ACT.Copy).then_inc(m_copied, 1)

            rounds(act, step)

            def residual(at):
                if (T := at(STD_LAG)) is not None:
                    r = T % RING
                    act.wait_ge(var_made, T + 1)
                    act.activation(std[r][:], stats[r][:, 7:8], ACT.Sqrt, bias=eps[:]).then_inc(std_made, 1)
                if (T := at(0)) is not None:
                    act.wait_ge(att_turned, T + 1)
                    act.activation(attT_hi[T % RING], ps[:, T % 2, 0:D].rearrange("p (k n) -> p k n", k=KD), ACT.Copy
                                   ).then_inc(attT_copied, 1)
                if (T := at(X1_LAG)) is not None:
                    act.wait_ge(x1_turned, T + 1)
                    act.activation(x1T[T % RING], ps[:, 4 + T % 2, 0:D].rearrange("p (k n) -> p k n", k=KD), ACT.Copy
                                   ).then_inc(x1T_copied, 1)

            tile_rounds(residual)

            act.wait_ge(logits_clipped, 1)
            act.activation(route[2], route[1], ACT.Sigmoid).then_inc(probs_made, 1)

            def expert(s, par, shared):
                if inside(s, 0):
                    act.wait_ge(fx_turned, s + 1)
                    act.activation(xh[par], ps[:, 0, 0:D].rearrange("p (k n) -> p k n", k=KD), ACT.Copy
                                   ).then_inc(fx_high, 1)
                if inside(s, DOWN_LAG):
                    act.wait_ge(h_turned, s - DOWN_LAG + 1)
                    act.activation(hh, h_banks, ACT.Copy).then_inc(h_high, 1)
                if inside(s, UP_LAG):
                    t = s - UP_LAG
                    act.wait_ge(gate_up, t + 1)
                    wait(act, h_made, t)
                    act.activation(f_s.rearrange("p (a n) -> p a n", a=2), ps[:, 1:3, 0:PIECE], ACT.Silu).then_inc(silu_made, 1)

            def check(a, b):
                act.wait_ge(sum_kept, b)
                act.activation(std_all[:, a:b], res[:, a:b, D], ACT.Sqrt, bias=eps[:]).then_inc(stds_made, 1)

            ffn_steps(act, expert, check)

        @block.vector
        def _(v):
            for q in range(2):
                v.memset(k_st[q][SR:SM], 1.0).then_inc(ones_rows, 1)
            v.wait_ge(consts_in, 16 * 6)

            def low_parts(i, par):
                b = 2 * i + par
                for k in range(KD):
                    v.wait_ge(xT_copied, KD * b + k + 1)
                    v.tensor_tensor(xT_lo[par][:, k], ps[:, k], xT_hi[par][:, k].bitcast(F32), ALU.subtract
                                    ).then_inc(xT_low, 1)

            def project(i, par):
                b = 2 * i + par
                for m in range(5):
                    if m < 4:
                        n = 4 * b + m
                        v.wait_ge(qk_read, 2 * (n + 1))
                        wait(v, low_made, n - AR + 1)
                        v.tensor_tensor(rest[m], qk32[m], parts[m][:, 0], ALU.subtract).then_inc(rest_made, 1)
                    if m:
                        v.wait_ge(mid_made, 4 * b + m)
                        v.tensor_tensor(parts[m - 1][:, 2], rest[m - 1], parts[m - 1][:, 1], ALU.subtract
                                        ).then_inc(low_made, 1)
                v.wait_ge(v_projected, b + 1)
                dst = v_all[:, bass.ds(b, 1)].rearrange("p o (a n) c -> p (o a) n c", a=2)
                for a in range(2):
                    v.tensor_tensor(dst[:, a], ps[:, 6 + a].rearrange("p (n c) -> p n c", n=2),
                                    bv.unsqueeze(1).broadcast_to([P, 2, D]), ALU.add).then_inc(v_kept, 1)

            batches(v, low_parts, project)

            def step(b, s):
                if (t := item(b, s, 0)):
                    g, q, u = NQ * t[0] + t[1] // U, t[1] // U, t[1] % U
                    i, h, n = M_UNITS[u]
                    w = (i + 1) * P
                    v.wait_ge(max_scored, U * g + u + 1)
                    if u == 0:
                        wait(v, m_split, g - 1)
                    nm = negmax[q % 2][:].rearrange("p (h t) -> p h t", h=QH)
                    v.tensor_reduce(nm[:, h:h + n, i:i + 1], ps[:, t[1] % SLOTS, 0:n * w].rearrange("p (h n) -> p h n", h=n),
                                    AX_X, ALU.max, negate=True).then_inc(max_found, 1)
                if (t := item(b, s, O_TURN + 1)) and t[1] % U == 0:
                    bb, q = t[0], t[1] // U
                    g = NQ * bb + q
                    v.wait_ge(o_turned, g + 2)
                    o = ps[:, 7].rearrange("p (t h d) -> p t h d", t=NT, h=QH)
                    v.reciprocal(rden[:].rearrange("p (t h) -> p t h", t=NT), o[:, :, :, DH]).then_inc(rden_made, 1)
                    v.wait_ge(rden_made, g + 1)
                    dst = res[:, bass.ds(NT * bb, NT), q * QH * DH:(q + 1) * QH * DH]
                    v.tensor_tensor(dst.rearrange("p t (h d) -> p t h d", h=QH), o[:, :, :, 0:DH],
                                    rden[:].rearrange("p (t h) -> p t h", t=NT).unsqueeze(3)
                                    .broadcast_to([P, NT, QH, DH]), ALU.mult).then_inc(att_kept, 1)

            rounds(v, step)


            def residual(at):
                if (T := at(STD_LAG)) is not None:
                    st = stats[T % RING]
                    v.wait_ge(stats_made, T + 1)
                    v.bn_aggr(st[:, 6:8], st[:, 0:6]).then_inc(var_made, 1)
                if (T := at(LOW_LAG)) is not None:
                    v.wait_ge(attT_copied, T + 1)
                    v.tensor_tensor(attT_lo[T % RING], ps[:, T % 2, 0:D].rearrange("p (k n) -> p k n", k=KD),
                                    attT_hi[T % RING].bitcast(F32), ALU.subtract).then_inc(attT_low, 1)
                old = at(NORM_LAG)
                if old is not None:
                    r = old % RING
                    v.wait_ge(std_made, old + 1)
                    v.reciprocal(rstd[r][:], std[r][:]).then_inc(rstd_made, 1)
                if (T := at(PROJ_LAG)) is not None:
                    v.wait_ge(xb_made, T // NT + 1)
                    v.wait_ge(out_projected, T + 1)
                    v.tensor_tensor(hid[T % RING], ps[:, 2 + T % 2, 0:D], xb[:, T], ALU.add).then_inc(sum_made, 1)
                if old is not None:
                    v.wait_ge(rstd_made, old + 1)
                    v.tensor_scalar(res[:, old, 0:D], hid[r], stats[r][:, 6:7], rstd[r][:], ALU.subtract, ALU.mult
                                    ).then_inc(x1_made, 1)
                if T is not None:
                    v.wait_ge(sum_made, T + 1)
                    v.bn_stats(stats[T % RING][:, 0:6], hid[T % RING]).then_inc(stats_made, 1)

            tile_rounds(residual)

            def turned_low(s, par):
                v.wait_ge(fx_high, s + 1)
                v.tensor_tensor(xl[par], ps[:, 0, 0:D].rearrange("p (k n) -> p k n", k=KD), xh[par].bitcast(F32),
                                ALU.subtract).then_inc(fx_low, 1)

            steps = [0]

            def link(ins):
                steps[0] += 1
                ins.then_inc(route_step, 1)
                v.wait_ge(route_step, steps[0])

            def over_e(c):
                return c.unsqueeze(2).broadcast_to([P, TT, E])

            def over_t(c):
                return c.unsqueeze(1).broadcast_to([P, TT, E])

            r0, r1, r2, desc, r4, onehot = route
            v.wait_ge(logits_made, TT)
            link(v.tensor_tensor(r0, ps[:, 6, 0:TE].rearrange("p (t e) -> p t e", t=TT), over_t(br[:]), ALU.add))
            v.tensor_scalar(r1, r0, 50.0, -50.0, ALU.min, ALU.max).then_inc(logits_clipped, 1)
            v.wait_ge(probs_made, 1)
            v.wait_ge(iotas_made, 3)
            link(v.tensor_reduce(col[0], r2, AX_X, ALU.max))
            link(v.tensor_tensor(r0, r2, over_e(col[0]), ALU.is_equal))
            link(v.tensor_tensor(r4, r0, desc, ALU.mult))
            link(v.tensor_reduce(col[1], r4, AX_X, ALU.max))
            link(v.tensor_tensor(onehot, r4, over_e(col[1]), ALU.is_equal))
            v.tensor_copy(onehot_bf, onehot.rearrange("p t e -> p (t e)")).then_inc(onehot_made, 1)
            turned_low(0, 0)
            link(v.tensor_scalar(col[2], col[0], 1.0 - 1e-8, 1e-8, ALU.min, ALU.max))
            link(v.tensor_scalar(col[1], col[2], 0.5, 1e-8, ALU.add, ALU.add))
            link(v.tensor_scalar(col[3], col[1], 2.0, 0.5, ALU.min, ALU.max))
            link(v.reciprocal(col[0], col[3]))
            link(v.tensor_scalar(share[:], col[0], 0.5, None, ALU.mult))
            link(v.tensor_tensor(res[:, 0:TT, D], col[2], col[0], ALU.mult))
            v.wait_ge(counted, 1)
            count, tiles, end, start = [stats[i][:, 0:E] for i in range(4)]
            link(v.tensor_reduce(count, ps[:, 7, 0:TE].rearrange("p (t e) -> p e t", t=TT), AX_X, ALU.add))
            link(v.tensor_tensor(need, count.unsqueeze(2).broadcast_to([P, E, TT]), step128, ALU.is_gt))
            link(v.tensor_reduce(end, need, AX_X, ALU.add))
            link(v.tensor_scalar(tiles, end, 1.0, None, ALU.max))
            link(v.tensor_copy(end, tiles))
            for e in range(1, E):
                link(v.tensor_tensor(end[:, e:e + 1], end[:, e - 1:e], tiles[:, e:e + 1], ALU.add))
            link(v.tensor_tensor(start, end, tiles, ALU.subtract))
            link(v.tensor_scalar(start, start, float(P), None, ALU.mult))
            link(v.tensor_scalar(ends[:], end[0:1], float(TT), None, ALU.add))
            link(v.tensor_tensor(r0, ps[:, 5, 0:TE].rearrange("p (t e) -> p t e", t=TT), over_t(start), ALU.add))
            link(v.tensor_tensor(r1, r0, onehot, ALU.mult))
            link(v.tensor_reduce(col[1], r1, AX_X, ALU.add))
            link(v.tensor_copy(pos[:], col[1]))
            link(v.tensor_tensor(tile_ge, tile_no, end[0:1].unsqueeze(1).broadcast_to([1, RT, E]), ALU.is_ge))
            link(v.tensor_reduce(tile_e, tile_ge[:, :, 0:E - 1], AX_X, ALU.add))
            v.tensor_scalar(tile_expert[:], tile_e, 1.0, None, ALU.add).then_inc(routed, 1)

            def row(T):
                return res[:, bass.ds(T, 1), 0:D].rearrange("p o c -> p (o c)")

            def expert(s, par, shared):
                add = inside(s, SUM_LAG)
                sorted_ = add and not shared(SUM_LAG)
                t = s - SUM_LAG
                if add:
                    v.wait_ge(y_made, t + 1)
                if add and not sorted_:
                    v.wait_ge(scattered[1 - par], 16 * (t // 2 + 1) if isinstance(t, int) else 8 * (t - (1 - par)) + 16)
                    v.scalar_tensor_tensor(row(t), ps[:, 7, 0:D], share[:, bass.ds(t, 1)], row(t), ALU.mult, ALU.add
                                           ).then_inc(y_read, 1)
                if sorted_:
                    n = t - TT
                    rest_ = f_rest[1 - par]
                    if isinstance(s, int) and n == 0:
                        v.wait_ge(rest_scattered, 16 * TT)
                    v.wait_ge(f_rest_in[1 - par], 16 * (n // 2 + 1) if isinstance(n, int) else 8 * (n - (1 - par)) + 16)
                    v.scalar_tensor_tensor(f_sum[1 - par], ps[:, 7, 0:D], rest_[:, D:D + 1], rest_[:, 0:D], ALU.mult, ALU.add
                                           ).then_inc(y_read, 1)
                    v.tensor_copy(res[:, bass.ds(n, 1), D + 1:RW].rearrange("p o c -> p (o c)").bitcast(I32),
                                  rest_[:, D + 1:RW].bitcast(I32))
                if inside(s, 0) and not (isinstance(s, int) and s == 0):
                    turned_low(s, par)
                if sorted_:
                    v.wait_ge(y_read, t + 1)
                    v.bn_stats(stats[1 - par][:, 0:6], f_sum[1 - par]).then_inc(sum_stats, 1)
                    v.wait_ge(sum_stats, n + 1)
                if inside(s, DOWN_LAG):
                    v.wait_ge(h_high, s - DOWN_LAG + 1)
                    k = KI - 1
                    v.tensor_tensor(hl[:, 0:k], h_banks[:, 0:k], hh[:, 0:k].bitcast(F32), ALU.subtract)
                    v.tensor_tensor(hh[LAST:P, k], h_banks[LAST:P, k], hh[LAST:P, k].bitcast(F32), ALU.subtract).then_inc(h_low, 1)
                if sorted_:
                    v.bn_aggr(stats[1 - par][:, 6:8], stats[1 - par][:, 0:6]).then_inc(sum_stats2, 1)
                    v.wait_ge(sum_stats2, n + 1)
                    v.tensor_scalar(row(n), f_sum[1 - par], stats[1 - par][:, 6:7], None, ALU.subtract)
                    v.tensor_scalar(res[:, bass.ds(n, 1), D:D + 1].rearrange("p o c -> p (o c)"), stats[1 - par][:, 7:8],
                                    1.0, None, ALU.mult).then_inc(sum_kept, 1)
                if inside(s, UP_LAG):
                    u = s - UP_LAG
                    v.wait_ge(lin_up, u + 1)
                    v.wait_ge(silu_made, u + 1)
                    wait(v, h_turned, u - 1)
                    v.tensor_tensor(f_h[1 - par][:, I:], f_s[:, I - LAST:I], ps[:, 4, PIECE - LAST:PIECE], ALU.mult)
                    v.tensor_tensor(f_h[1 - par][:, 0:I].rearrange("p (a n) -> p a n", a=2), f_s.rearrange("p (a n) -> p a n", a=2),
                                    ps[:, 3:5, 0:PIECE], ALU.mult).then_inc(h_made, 1)

            def check(a, b):
                c = CHECKS.index(b) + 1
                v.wait_ge(stds_made, c)
                v.reciprocal(std_all[:, a:b], std_all[:, a:b]).then_inc(rstds_made, 1)
                v.wait_ge(rstds_made, c)
                for t in range(a, b):
                    v.tensor_scalar(res[:, t, 0:D], res[:, t, 0:D], std_all[:, t:t + 1], None, ALU.mult).then_inc(normed, 1)

            ffn_steps(v, expert, check)

        @block.tensor
        def _(pe):
            pe.sem_inc(pv_done, NT)
            pe.sem_inc(o_turned, 1)
            pe.wait_ge(consts_made, 2)

            def turn(i, par):
                b = 2 * i + par
                pe.wait_ge(x_loaded[par], 16 * (i + 1))
                wait(pe, xT_low, KD * b)
                for k in range(KD):
                    for n in range(NT):
                        mm = pe.transpose(ps[:, k, n * P:(n + 1) * P], x_in[par][:, n, k * P:(k + 1) * P], ident[:])
                mm.then_inc(x_turned, 1)

            def project(i, par):
                b = 2 * i + par
                if isinstance(b, int) and b == 0:
                    pe.wait_ge(wqkv_split, 2)
                pe.wait_ge(xT_low, KD * (b + 1))
                w_hi, w_lo = (w.rearrange("p (k n) -> p k n", k=KD) for w in (wqkv_hi, wqkv_lo))
                passes = ((xT_hi[par], w_hi), (xT_lo[par], w_hi), (xT_hi[par], w_lo))
                for m in range(4):
                    wait(pe, qk_read, 2 * (4 * b + m - 3))
                    for k in range(KD):
                        for i, (xp, wp) in enumerate(passes):
                            mm = pe.matmul(ps[:, 2 + m], wp[:, k, m * P:(m + 1) * P], xp[:, k],
                                           start=k == 0 and i == 0, stop=k == KD - 1 and i == 2)
                    mm.then_inc(qk_projected, 1)
                wait(pe, v_kept, 2 * b)
                for n in range(NT):
                    for k in range(KD):
                        for i, (xp, wp) in enumerate(passes):
                            mm = pe.matmul(ps[:, 6 + n // 2, (n % 2) * D:(n % 2 + 1) * D], xp[:, k, n * P:(n + 1) * P],
                                           wp[:, k, 2 * D:3 * D], start=k == 0 and i == 0, stop=k == KD - 1 and i == 2)
                mm.then_inc(v_projected, 1)

            batches(pe, turn, project)

            pe.wait_ge(consts_made, 4)
            pe.wait_ge(v_kept, 2 * B)
            pe.wait_ge(qk_read, 8 * B)
            pe.wait_ge(ones_rows, 2)

            def step(b, s):
                if (t := item(b, s, 0)):
                    g, q, u = NQ * t[0] + t[1] // U, t[1] // U, t[1] % U
                    i, h0, n = M_UNITS[u]
                    w = (i + 1) * P
                    if u == 0:
                        pe.wait_ge(stack_loaded[q], 16 * 2 * NP_ * (t[0] + 1))
                    if not isinstance(g, int) or U * g + u >= SLOTS:
                        pe.wait_ge(max_found, U * g + u + 1 - SLOTS)
                    for a in range(n):
                        dst = ps[:, t[1] % SLOTS, a * w:(a + 1) * w]
                        pe.matmul(dst, q_st[q][0:SR, h0 + a, i * P:w], k_st[q][0:SR, h0 + a, 0:w], start=True, stop=False)
                        mm = pe.matmul(dst[:, i * P:w], ident_bf[:], mask_q[:], start=False, stop=True)
                    mm.then_inc(max_scored, 1)
                if (t := item(b, s, S_LAG)):
                    g, q, u = NQ * t[0] + t[1] // U, t[1] // U, t[1] % U
                    j, h0, n = S_UNITS[u]
                    w = S - j * P
                    if u == 0:
                        pe.wait_ge(m_placed, 16 * (g + 1))
                        if isinstance(g, int) and g == 2:
                            pe.wait_ge(ones_rows, NQ)
                    pe.wait_ge(exped, U * g + u + 1)
                    for a in range(n):
                        mm = pe.matmul(ps[:, 3 + t[1] % SLOTS, a * w:(a + 1) * w], k_st[q][0:SM, h0 + a, j * P:(j + 1) * P],
                                       q_st[q][0:SM, h0 + a, j * P:S], start=True, stop=True)
                    mm.then_inc(scored, 1)
                if (t := item(b, s, PV_LAG)) and t[1] % U in S_LAST:
                    g, q, j = NQ * t[0] + t[1] // U, t[1] // U, S_LAST[t[1] % U]
                    pe.wait_ge(masked, NT * g + j + 1)
                    if j == 0:
                        if isinstance(g, int) and g == 0:
                            pe.wait_ge(v_ones, 2)
                        pe.wait_ge(v_ready, g + 1)
                        pe.wait_ge(o_copied, g + 1)
                    for h in range(QH):
                        mm = pe.matmul(ps[32 * h:32 * h + 32, 6, j * P:S], v_ext[q % 2][:, j, h],
                                       probs[j][:, h], start=j == 0, stop=j == NT - 1)
                    mm.then_inc(pv_done, 1)
                if (t := item(b, s, M_TURN)) and t[1] % U == 0:
                    g = NQ * t[0] + t[1] // U
                    pe.wait_ge(m_split, g + 1)
                    wait(pe, att_kept, g - 1)
                    pe.transpose(ps[:, 7, 0:P // 2].bitcast(BF16), m_parts[:], ident_bf[:]).then_inc(m_turned, 1)
                if (t := item(b, s, O_TURN)) and t[1] % U == 0:
                    g = NQ * t[0] + t[1] // U
                    pe.wait_ge(o_copied, g + 2)
                    wait(pe, att_kept, g)
                    pe.wait_ge(m_copied, min(g + 2, QUADS) if isinstance(g, int) else g + 2)
                    for n in range(NT):
                        mm = pe.transpose(ps[:, 7, n * P:(n + 1) * P], o_sb[:, n * P:(n + 1) * P], ident[:])
                    mm.then_inc(o_turned, 1)

            rounds(pe, step)

            pe.wait_ge(att_kept, QUADS)
            pe.wait_ge(wo_split, 2)

            def residual(at):
                if (T := at(0)) is not None:
                    wait(pe, attT_low, T - 1)
                    for k in range(KD):
                        mm = pe.transpose(ps[:, T % 2, k * P:(k + 1) * P], res[:, T, k * P:(k + 1) * P], ident[:])
                    mm.then_inc(att_turned, 1)
                if (T := at(PROJ_LAG)) is not None:
                    pe.wait_ge(attT_low, T + 1)
                    wait(pe, sum_made, T - 1)
                    passes = ((attT_hi[T % RING], wo_hi), (attT_lo[T % RING], wo_hi), (attT_hi[T % RING], wo_lo))
                    for k in range(KD):
                        for i, (ap, wp) in enumerate(passes):
                            mm = pe.matmul(ps[:, 2 + T % 2, 0:D], ap[:, k], wp[:, k],
                                           start=k == 0 and i == 0, stop=k == KD - 1 and i == 2)
                    mm.then_inc(out_projected, 1)
                if (T := at(X1_LAG)) is not None:
                    pe.wait_ge(x1_made, T + 1)
                    wait(pe, x1T_copied, T - 1)
                    for k in range(KD):
                        mm = pe.transpose(ps[:, 4 + T % 2, k * P:(k + 1) * P], res[:, T, k * P:(k + 1) * P], ident[:])
                    mm.then_inc(x1_turned, 1)
                if (T := at(LOGIT_LAG)) is not None:
                    pe.wait_ge(x1T_copied, T + 1)
                    for k in range(KD):
                        mm = pe.matmul(ps[:, 6, T * E:(T + 1) * E], x1T[T % RING][:, k], wr[:, k], start=k == 0, stop=k == KD - 1)
                    mm.then_inc(logits_made, 1)

            tile_rounds(residual)

            def rank_tokens():
                pe.wait_ge(onehot_made, 1)
                pe.matmul(ps[:, 5, 0:TE], before[:], onehot_bf, start=True, stop=False)
                for T in range(TT - 1):
                    left = TT - 1 - T
                    pe.matmul(ps[:, 5, (T + 1) * E:TE].rearrange("p (t e) -> p t e", t=left), ones_bf[:],
                              onehot_bf[:, T * E:(T + 1) * E].unsqueeze(1).broadcast_to([P, left, E]),
                              start=False, stop=T == TT - 2)
                pe.matmul(ps[:, 7, 0:TE], ones_bf[:], onehot_bf, start=True, stop=True).then_inc(counted, 1)

            rank_tokens()

            pe.wait_ge(split_done, 1)
            pe.wait_ge(x1T_copied, TT)

            def tile_set(t, lag, shared):
                if shared(lag):
                    return 0, 0
                w = pe.value_load(tile_expert[0:1, bass.ds(t - TT, 1)], min_val=1, max_val=E)
                return w, w % 2 * WBUF

            def expert(s, par, shared):
                if isinstance(s, int) and s == DOWN_LAG:
                    pe.wait_ge(routed, 1)
                if inside(s, 0):
                    pe.wait_ge(fx_loaded[par], 8 * (s - par) + 16)
                    wait(pe, fx_low, s)
                    for k in range(KD):
                        mm = pe.transpose(ps[:, 0, k * P:(k + 1) * P], f_x[par][:, k * P:(k + 1) * P], ident[:])
                    mm.then_inc(fx_turned, 1)
                if inside(s, DOWN_LAG):
                    t = s - DOWN_LAG
                    pe.wait_ge(h_made, t + 1)
                    wait(pe, h_low, t)
                    for k in range(KI):
                        mm = pe.transpose(ps[:, 5 + k // 4, k % 4 * P:(k % 4 + 1) * P], f_h[par][:, k * P:(k + 1) * P], ident[:])
                    mm.then_inc(h_turned, 1)
                if inside(s, UP_LAG):
                    t = s - UP_LAG
                    w, at = tile_set(t, UP_LAG, shared)
                    if not shared(UP_LAG):
                        pe.wait_ge(split_done, w + 1)
                    pe.wait_ge(fx_low, t + 1)
                    x_hi, x_lo = xh[1 - par], xl[1 - par]
                    for half, bank, read, made in ((0, 1, silu_made, gate_up), (1, 3, h_made, lin_up)):
                        wait(pe, read, t)
                        for k in range(KD):
                            for i, (xp, low) in enumerate(((x_hi, 0), (x_hi, SLOT), (x_lo, 0))):
                                for a in range(2):
                                    mm = pe.matmul(ps[:, bank + a, 0:PIECE], xp[:, k],
                                                   w_split[:, bass.ds(at + low + k * UP + half * I + a * PIECE, PIECE)],
                                                   start=k == 0 and i == 0, stop=k == KD - 1 and i == 2)
                        mm.then_inc(made, 1)
                if inside(s, DOWN_LAG):
                    t = s - DOWN_LAG
                    _, at = tile_set(t, DOWN_LAG, shared)
                    pe.wait_ge(h_low, t + 1)
                    wait(pe, y_read, t)
                    for k in range(KI - 1):
                        for i, (hp, low) in enumerate(((hh, 0), (hh, SLOT), (hl, 0))):
                            mm = pe.matmul(ps[:, 7, 0:D], hp[:, k], w_split[:, bass.ds(at + low + UPW + k * D, D)],
                                           start=k == 0 and i == 0, stop=False)
                    k = KI - 1
                    mm = pe.matmul(ps[:, 7, 0:D], hh[:, k], w_split[:, bass.ds(at + UPW + k * D, D)], start=False, stop=False)
                    mm = pe.matmul(ps[:, 7, 0:D], hh[0:LAST, k], w_split[0:LAST, bass.ds(at + SLOT + UPW + k * D, D)],
                                   start=False, stop=True)
                    mm.then_inc(y_made, 1)

            ffn_steps(pe, expert)


def kernel(**inputs):
    import numpy as np
    import concourse.bacc as bacc
    from concourse import mybir as mb
    from concourse.bass_utils import run_bass_kernel_spmd

    a = {k.replace("L0_", ""): np.asarray(t) for k, t in inputs.items()}

    def by_rows(w):
        return w.reshape(*w.shape[:-2], -1, P, w.shape[-1]).swapaxes(-3, -2)

    def on_all(t):
        return np.broadcast_to(t, (P, t.size))

    sets = {}
    for n in (1, 2, 3):
        w = np.concatenate([a[f"ffn_sw{n}"][None], a[f"ffn_ew{n}"]])
        sets[n] = w.transpose(0, 2, 1)
    up = by_rows(np.concatenate([sets[1], sets[3]], axis=2)).reshape(NW, P, UPW)
    down = np.zeros((NW, KI * P, D), np.float32)
    down[:, :I] = sets[2]
    down[:, I:] = down[:, I - LAST:I]
    down = by_rows(down).reshape(NW, P, DNW)
    laid = {
        "x": a["attn_x"].reshape(TT, P, D),
        "w_qkv": by_rows(np.concatenate([a["attn_w_q"], a["attn_w_k"], a["attn_w_v"]], axis=1)),
        "b_qk": np.concatenate([a["attn_b_q"], a["attn_b_k"]]).reshape(4, P).T,
        "b_v": on_all(a["attn_b_v"]),
        "w_o": by_rows(a["attn_w_o"]),
        "b_o": on_all(a["attn_b_o"]),
        "w_r": by_rows(a["ffn_router_w"].T),
        "b_r": on_all(a["ffn_routing_bias"]),
        "w_sets": np.concatenate([up, down], axis=2),
    }
    nc = bacc.Bacc("TRN2", target_bir_lowering=False, num_devices=1)
    arrays, args = {}, {}
    for name, t in laid.items():
        arrays[f"in_{name}"] = np.ascontiguousarray(t)
        args[name] = nc.dram_tensor(f"in_{name}", t.shape, mb.dt.float32, kind="ExternalInput").ap()
    out = nc.dram_tensor("out_rows", (TOK, D), mb.dt.float32, kind="ExternalOutput").ap()
    block_kernel(nc, **args, out=out)
    r = run_bass_kernel_spmd(nc, [arrays], core_ids=[0])
    return r.results[0]["out_rows"].reshape(B, S, D)
```
